# Optimizing a Trainium2 kernel written in Bass

```python
import numpy as np
import jax
import jax.numpy as jnp

def _softmax(x, axis=-1):
    return jax.nn.softmax(x, axis=axis)

def _gelu(x):
    return jax.nn.gelu(x, approximate=True)

def _silu(x):
    return jax.nn.silu(x)

def _sigmoid(x):
    return jax.nn.sigmoid(x)

def _layernorm(x, axis=-1, eps=1e-05):
    m = jnp.mean(x, axis=axis, keepdims=True)
    v = jnp.var(x, axis=axis, keepdims=True)
    return (x - m) / jnp.sqrt(v + eps)

def _scatter_add(tgt, idx, src, axis=0):
    return tgt.at[idx].add(src)

def _segment_sum(src, seg, n):
    return jax.ops.segment_sum(src, seg, n)
kernel_name = 'mk_conv_preact_d2_conv_nchw256_r4_310a32'

def setup_inputs(seed: int=0):
    np.random.seed(seed)
    _w = jnp.asarray

    def _rec_inputs():
        import jax
        import jax.numpy as jnp
        _gk = jax.random.key(seed)
        x = 7.22e-05 + 1 * jax.random.normal(jax.random.fold_in(_gk, 1), (8, 64, 16, 16), jnp.float32)
        return x
    x = _rec_inputs()

    def _L0_conv_setup():
        import jax, jax.numpy as jnp
        import numpy as np
        KSIZE, STRIDE, RATE, FUSE_K, SOFTMAX_SCALE = (3, 1, 2, 3, 10.0)
        ESCAPE_NAN = 0.0001

        def _extract_patches(x, ksize, stride, pad):
            x = jnp.pad(x, ((0, 0), (0, 0), (pad, pad), (pad, pad)))
            N, C, H, W = x.shape
            oh = (H - ksize) // stride + 1
            ow = (W - ksize) // stride + 1
            cols = [x[:, :, di:di + oh * stride:stride, dj:dj + ow * stride:stride] for di in range(ksize) for dj in range(ksize)]
            p = jnp.stack(cols, axis=2)
            p = p.reshape(N, C, ksize, ksize, oh * ow)
            return p.transpose(0, 4, 1, 2, 3)

        def _fuse_conv(y, k):
            ker = jnp.eye(k, dtype=y.dtype).reshape(1, 1, k, k)
            pad = k // 2
            return jax.lax.conv_general_dilated(y[:, None], ker, (1, 1), [(pad, pad), (pad, pad)], dimension_numbers=('NCHW', 'OIHW', 'NCHW'))[:, 0]

        def _contextual_attention(f, mask):
            N, C, H, W = f.shape
            kernel = 2 * RATE
            raw_w = _extract_patches(f, kernel, RATE * STRIDE, pad=1)
            fd = f[:, :, ::RATE, ::RATE]
            Hd, Wd = (fd.shape[2], fd.shape[3])
            L = Hd * Wd
            w = _extract_patches(fd, KSIZE, STRIDE, pad=1)
            md = mask[0:1, :, ::RATE, ::RATE]
            m = _extract_patches(md, KSIZE, STRIDE, pad=1)[0]
            mm = (jnp.mean(m, axis=(1, 2, 3)) == 0.0).astype(f.dtype)
            norm = jnp.sqrt(jnp.sum(w * w, axis=(2, 3, 4), keepdims=True))
            wn = w / jnp.maximum(norm, ESCAPE_NAN)
            fp = _extract_patches(fd, KSIZE, STRIDE, pad=1)
            yi = jnp.einsum('npckl,nqckl->nqp', fp, wn)
            yi = _fuse_conv(yi, FUSE_K)
            yi = yi.reshape(N, Hd, Wd, Hd, Wd).transpose(0, 2, 1, 4, 3).reshape(N, L, L)
            yi = _fuse_conv(yi, FUSE_K)
            yi = yi.reshape(N, Wd, Hd, Wd, Hd).transpose(0, 2, 1, 4, 3).reshape(N, L, L)
            yi = yi * mm[None, :, None]
            yi = jax.nn.softmax(yi * SOFTMAX_SCALE, axis=1)
            yi = yi * mm[None, :, None]
            yi = yi.reshape(N, L, Hd, Wd)

            def deconv_one(y1, rw):
                wt = jnp.flip(rw, (2, 3)).transpose(1, 0, 2, 3)
                pad = kernel - 1 - 1
                return jax.lax.conv_general_dilated(y1[None], wt, (1, 1), [(pad, pad), (pad, pad)], lhs_dilation=(RATE, RATE), dimension_numbers=('NCHW', 'OIHW', 'NCHW'))[0]
            out = jax.vmap(deconv_one)(yi, raw_w) / 4.0
            return out

        def _forward(feature, mask):
            N, C, H, W = feature.shape
            mw = mask.shape[2]
            s = mw // H
            m = jax.lax.reduce_window(mask, 0.0, jax.lax.add, (1, 1, 2, 2), (1, 1, s, s), 'VALID') / 4.0
            m = jnp.round(m)
            return _contextual_attention(feature, m)
        key = jax.random.key(seed)
        k1, _ = jax.random.split(key)
        feature = jax.random.normal(k1, (8, 64, 16, 16), dtype=jnp.float32)
        mask = jnp.zeros((8, 1, 32, 32), dtype=jnp.float32)
        mask = mask.at[:, :, 40:22, 40:22].set(1.0)
        return {'feature': feature, 'mask': mask}
    _L0_conv_all = _L0_conv_setup()
    _L0_conv_in = {k: v for k, v in _L0_conv_all.items() if k in ('mask',)}
    del _L0_conv_all

    def _L1_conv_setup():
        import jax, jax.numpy as jnp
        import numpy as np
        OOC, OIC, K1, K2 = (16, 16, 3, 3)
        R0, R1 = (4, 4)

        def _build_weight(weight, alphas, betas):
            a = alphas.reshape(R0, R1)[:, :, None, None, None, None]
            b = betas.reshape(R0, R1)[:, :, None, None, None, None]
            w = weight[None, None]
            act = w * a / (1.0 + jnp.exp(w * b))
            return act.transpose(0, 2, 1, 3, 4, 5).reshape(R0 * OOC, R1 * OIC, K1, K2)
        key = jax.random.key(seed)
        k0, k1, k2, k3, k4 = jax.random.split(key, 5)
        x = jax.random.normal(k0, (32, 64, 56, 56), dtype=jnp.float32)
        wb = float(np.sqrt(6.0 / (OIC * K1 * K2 + OOC * K1 * K2)))
        weight = jax.random.uniform(k1, (OOC, OIC, K1, K2), minval=-wb, maxval=wb, dtype=jnp.float32)
        ab = float(np.sqrt(6.0 / (1 + R0 * R1)))
        alphas = jax.random.uniform(k2, (1, R0 * R1), minval=-ab, maxval=ab, dtype=jnp.float32)
        betas = jax.random.uniform(k3, (1, R0 * R1), minval=-ab, maxval=ab, dtype=jnp.float32)
        bias = jax.random.normal(k4, (64,), dtype=jnp.float32) * 0.01
        return {'x': x, 'weight': weight, 'alphas': alphas, 'betas': betas, 'bias': bias}
    _L1_conv_all = _L1_conv_setup()
    _L1_conv_in = {k: v for k, v in _L1_conv_all.items() if k in ('weight', 'alphas', 'betas', 'bias')}
    del _L1_conv_all
    return {'x': x, 'L0_conv_mask': _L0_conv_in['mask'], 'L1_conv_weight': _L1_conv_in['weight'], 'L1_conv_alphas': _L1_conv_in['alphas'], 'L1_conv_betas': _L1_conv_in['betas'], 'L1_conv_bias': _L1_conv_in['bias']}

def reference(x, L0_conv_mask, L1_conv_weight, L1_conv_alphas, L1_conv_betas, L1_conv_bias):
    import jax
    import jax.numpy as jnp

    def _L0_conv_ref(feature, mask):
        import jax, jax.numpy as jnp
        import numpy as np
        KSIZE, STRIDE, RATE, FUSE_K, SOFTMAX_SCALE = (3, 1, 2, 3, 10.0)
        ESCAPE_NAN = 0.0001

        def _extract_patches(x, ksize, stride, pad):
            x = jnp.pad(x, ((0, 0), (0, 0), (pad, pad), (pad, pad)))
            N, C, H, W = x.shape
            oh = (H - ksize) // stride + 1
            ow = (W - ksize) // stride + 1
            cols = [x[:, :, di:di + oh * stride:stride, dj:dj + ow * stride:stride] for di in range(ksize) for dj in range(ksize)]
            p = jnp.stack(cols, axis=2)
            p = p.reshape(N, C, ksize, ksize, oh * ow)
            return p.transpose(0, 4, 1, 2, 3)

        def _fuse_conv(y, k):
            ker = jnp.eye(k, dtype=y.dtype).reshape(1, 1, k, k)
            pad = k // 2
            return jax.lax.conv_general_dilated(y[:, None], ker, (1, 1), [(pad, pad), (pad, pad)], dimension_numbers=('NCHW', 'OIHW', 'NCHW'))[:, 0]

        def _contextual_attention(f, mask):
            N, C, H, W = f.shape
            kernel = 2 * RATE
            raw_w = _extract_patches(f, kernel, RATE * STRIDE, pad=1)
            fd = f[:, :, ::RATE, ::RATE]
            Hd, Wd = (fd.shape[2], fd.shape[3])
            L = Hd * Wd
            w = _extract_patches(fd, KSIZE, STRIDE, pad=1)
            md = mask[0:1, :, ::RATE, ::RATE]
            m = _extract_patches(md, KSIZE, STRIDE, pad=1)[0]
            mm = (jnp.mean(m, axis=(1, 2, 3)) == 0.0).astype(f.dtype)
            norm = jnp.sqrt(jnp.sum(w * w, axis=(2, 3, 4), keepdims=True))
            wn = w / jnp.maximum(norm, ESCAPE_NAN)
            fp = _extract_patches(fd, KSIZE, STRIDE, pad=1)
            yi = jnp.einsum('npckl,nqckl->nqp', fp, wn)
            yi = _fuse_conv(yi, FUSE_K)
            yi = yi.reshape(N, Hd, Wd, Hd, Wd).transpose(0, 2, 1, 4, 3).reshape(N, L, L)
            yi = _fuse_conv(yi, FUSE_K)
            yi = yi.reshape(N, Wd, Hd, Wd, Hd).transpose(0, 2, 1, 4, 3).reshape(N, L, L)
            yi = yi * mm[None, :, None]
            yi = jax.nn.softmax(yi * SOFTMAX_SCALE, axis=1)
            yi = yi * mm[None, :, None]
            yi = yi.reshape(N, L, Hd, Wd)

            def deconv_one(y1, rw):
                wt = jnp.flip(rw, (2, 3)).transpose(1, 0, 2, 3)
                pad = kernel - 1 - 1
                return jax.lax.conv_general_dilated(y1[None], wt, (1, 1), [(pad, pad), (pad, pad)], lhs_dilation=(RATE, RATE), dimension_numbers=('NCHW', 'OIHW', 'NCHW'))[0]
            out = jax.vmap(deconv_one)(yi, raw_w) / 4.0
            return out

        def _forward(feature, mask):
            N, C, H, W = feature.shape
            mw = mask.shape[2]
            s = mw // H
            m = jax.lax.reduce_window(mask, 0.0, jax.lax.add, (1, 1, 2, 2), (1, 1, s, s), 'VALID') / 4.0
            m = jnp.round(m)
            return _contextual_attention(feature, m)
        return _forward(feature, mask)

    def _L1_conv_ref(x, weight, alphas, betas, bias):
        import jax, jax.numpy as jnp
        import numpy as np
        OOC, OIC, K1, K2 = (16, 16, 3, 3)
        R0, R1 = (4, 4)

        def _build_weight(weight, alphas, betas):
            a = alphas.reshape(R0, R1)[:, :, None, None, None, None]
            b = betas.reshape(R0, R1)[:, :, None, None, None, None]
            w = weight[None, None]
            act = w * a / (1.0 + jnp.exp(w * b))
            return act.transpose(0, 2, 1, 3, 4, 5).reshape(R0 * OOC, R1 * OIC, K1, K2)
        W = _build_weight(weight, alphas, betas)
        out = jax.lax.conv_general_dilated(x, W, window_strides=(1, 1), padding=[(1, 1), (1, 1)], dimension_numbers=('NCHW', 'OIHW', 'NCHW'))
        return out + bias[None, :, None, None]

    def _gn(v, G=32, eps=1e-05):
        B_, C_, H_, W_ = v.shape
        g = v.reshape(B_, G, C_ // G, H_, W_)
        m = jnp.mean(g, axis=(2, 3, 4), keepdims=True)
        s = jnp.var(g, axis=(2, 3, 4), keepdims=True)
        return ((g - m) / jnp.sqrt(s + eps)).reshape(v.shape)

    def _ln_c(v, eps=1e-06):
        m = jnp.mean(v, axis=1, keepdims=True)
        s = jnp.var(v, axis=1, keepdims=True)
        return (v - m) / jnp.sqrt(s + eps)

    def _ln_t(v, eps=1e-05):
        m = jnp.mean(v, axis=-1, keepdims=True)
        s = jnp.var(v, axis=-1, keepdims=True)
        return (v - m) / jnp.sqrt(s + eps)

    def _to_tokens(v):
        B_, C_, H_, W_ = v.shape
        return v.reshape(B_, C_, H_ * W_).transpose(0, 2, 1)

    def _from_tokens(t, like):
        B_, C_, H_, W_ = like.shape
        return t.transpose(0, 2, 1).reshape(B_, C_, H_, W_)
    x = x + _L0_conv_ref(_gn(x), L0_conv_mask)
    x = x + _L1_conv_ref(_gn(x), L1_conv_weight, L1_conv_alphas, L1_conv_betas, L1_conv_bias)
    return x

_drawn_inputs = setup_inputs


def setup_inputs(seed=0):
    import zlib

    import numpy as np

    out = dict(_drawn_inputs(seed))
    spreads = {}
    factors = {'L1_conv_betas': 8.0, 'L1_conv_bias': 8.0}
    for name, (base, spread) in spreads.items():
        noise = np.random.default_rng([zlib.crc32(name.encode()), seed]).standard_normal(out[name].shape)
        drawn = base * np.exp(spread * noise) if base else spread * noise
        out[name] = jnp.asarray(drawn.astype(out[name].dtype))
    for name, factor in factors.items():
        out[name] = (out[name] * factor).astype(out[name].dtype)
    return out
```

```python
from contextlib import ExitStack

import concourse.bass as bass
from concourse import mybir
import numpy as np

N, C, H, W = 8, 64, 16, 16
HW = H * W
PAIRS = N // 2
UNITS, PPU = 2, 2
G = 8
L = G * G
P = 128
TAPS = 9
R = 4
OC = C // R
GN_EPS = 1e-5
MIN_NORM2 = 1e-8
ROUND = 1.5 * 2.0 ** 23
SHIFTS = [(0, 0), (0, 1), (0, -1), (1, 0), (-1, 0), (1, 1), (1, -1), (-1, 1), (-1, -1)]
MASK_SIDE = 32
COLUMN_SHIFTS = [(slice(1, G), slice(0, G - 1)), (slice(0, G), slice(0, G)), (slice(0, G - 1), slice(1, G))]
SCALE = 10.0

C_AVG, C_DIFF = 0, P
C_FUSE1 = 2 * P
C_FUSE2 = C_FUSE1 + 3 * P
C_SHIFT = C_FUSE2 + 3 * L
C_COLS = C_SHIFT + len(SHIFTS) * L
C_EYE = C_SHIFT


def constants():
    k = np.zeros((P, C_COLS), np.float32)
    for m in range(P):
        for p in (m, m ^ 1):
            k[p, C_AVG + m] = 0.5
            k[p, C_DIFF + m] = 0.5 if p == m else -0.5
    turn = np.arange(L).reshape(G, G).T.reshape(L)
    for d in (-1, 0, 1):
        for i in range(L):
            if 0 <= i + d < L:
                for h in range(2):
                    k[64 * h + i + d, C_FUSE1 + (d + 1) * P + 64 * h + i] = 1
                    k[64 * h + turn[i + d], C_FUSE2 + (d + 1) * L + turn[i]] = 1
    for n, (s, t) in enumerate(SHIFTS):
        for a in range(G):
            for b in range(G):
                if 0 <= a - s < G and 0 <= b - t < G:
                    for h in range(2):
                        k[64 * h + G * (a - s) + b - t, C_SHIFT + n * L + G * a + b] = 1
    return k


def build(nc, x, mask, weight, ab, bias, const, out):
    fp32 = mybir.dt.float32
    ALU = mybir.AluOpType
    ACT = mybir.ActivationFunctionType
    AX = mybir.AxisListType

    with ExitStack() as ctx:
        def sb(name, *shape):
            return ctx.enter_context(nc.sbuf_tensor(name, list(shape), fp32))

        def sem(name):
            return ctx.enter_context(nc.semaphore(name))

        x_sb = sb("x_sb", P, PAIRS, HW)
        k_sb = sb("k_sb", P, C_COLS)
        w_sb = sb("w_sb", P, TAPS, OC)
        ab_sb = sb("ab_sb", P, 2, R)
        bias_sb = sb("bias_sb", P, 1)
        mask_sb = sb("mask_sb", 1, MASK_SIDE * MASK_SIDE)
        ones = sb("ones", 1, P)
        mrow = sb("mrow", 1, G, G, 2)
        mcell = sb("mcell", 1, G, G)
        mpad = sb("mpad", 1, G + 2, G + 2)
        mh1 = sb("mh1", 1, G + 2, G)
        mh2 = sb("mh2", 1, G + 2, G)
        mv1 = sb("mv1", 1, G, G)
        mv2 = sb("mv2", 1, G, G)
        mm10 = sb("mm10", 1, L)
        keep10 = sb("keep10", P, L)
        keep4 = sb("keep4", P, L)
        wexp = sb("wexp", P, R, TAPS * OC)
        wden = sb("wden", P, R, TAPS * OC)
        wrec = sb("wrec", P, R, TAPS * OC)
        w_full = sb("w_full", P, TAPS, C)
        stats = sb("stats", P, 2, PAIRS, 6)
        mv = sb("mv", P, 2, PAIRS, 2)
        dif2 = sb("dif2", P, 2, PAIRS)
        gst = sb("gst", P, 2, UNITS, 4 * PPU)
        var = sb("var", P, 2, PAIRS)
        ln = sb("ln", P, 2, PAIRS)
        y0 = sb("y0", P, 2, PAIRS)
        ya = sb("ya", P, 2, PAIRS)
        yb = sb("yb", P, 2, PAIRS)
        rstd = sb("rstd", P, 2, PAIRS)
        f_sb = sb("f_sb", P, PAIRS, 4, L)
        fd = sb("fd", P, PAIRS, 3, G + 2, G)
        gdiag = sb("gdiag", P, PAIRS, L)
        n2 = sb("n2", P, PAIRS)
        n2c = sb("n2c", P, PAIRS)
        nln = sb("nln", P, PAIRS)
        ny0 = sb("ny0", P, PAIRS)
        nya = sb("nya", P, PAIRS)
        nyb = sb("nyb", P, PAIRS)
        rnorm = sb("rnorm", P, PAIRS)
        ypad = sb("ypad", P, PAIRS, L + 2)
        ext = sb("ext", P, PAIRS, (G + 2) * G)
        z = sb("z", P, PAIRS, L)
        nmax = sb("nmax", P, PAIRS)
        e_sb = sb("e_sb", P, PAIRS, L)
        esum = sb("esum", P, PAIRS)
        erec = sb("erec", P, PAIRS)
        ppad = sb("ppad", P, PAIRS, 3, G + 2, G)
        b_sb = sb("b_sb", P, PAIRS, 4, L)
        ft_sb = sb("ft_sb", P, PAIRS, 4, C)
        x1 = sb("x1", P, PAIRS, HW)
        x2 = sb("x2", P, PAIRS, H + 2, W + 2)
        o_sb = sb("o_sb", P, PAIRS, HW)

        bank = [ctx.enter_context(nc.psum_tensor(f"bank{i}", [P, 512], fp32)) for i in range(8)]


        x_in = [sem(f"x_in{u}") for u in range(UNITS)]
        gnk_in, fuse_in, shift_in, w_in, ab_in, bias_in, mask_in = map(sem, (
            "gnk_in", "fuse_in", "shift_in", "w_in", "ab_in", "bias_in", "mask_in"))
        stored = [sem(f"stored{u}") for u in range(UNITS)]
        pads_zero, ones_set, pool_step, dve_step, act_step = map(sem, (
            "pads_zero", "ones_set", "pool_step", "dve_step", "act_step"))
        mask_row, mask_bc, keep_ready = map(sem, ("mask_row", "mask_bc", "keep_ready"))
        wexp_ready, w_ready = map(sem, ("wexp_ready", "w_ready"))
        moments, groups, var_ready, gn_y0 = map(sem, ("moments", "groups", "var_ready", "gn_y0"))
        fd_ready, f_ready, gram_done, n2_ready, norm_y0, y_ready = map(sem, (
            "fd_ready", "f_ready", "gram_done", "n2_ready", "norm_y0", "y_ready"))
        y1_done, ext_ready, y2_done, z_ready, e_ready, p_ready = map(sem, (
            "y1_done", "ext_ready", "y2_done", "z_ready", "e_ready", "p_ready"))
        ft_done, ft_ready, b_done, b_ready, dec_done, x1_ready = map(sem, (
            "ft_done", "ft_ready", "b_done", "b_ready", "dec_done", "x1_ready"))
        x2_ready, conv_done, out_ready = map(sem, ("x2_ready", "conv_done", "out_ready"))

        block = ctx.enter_context(nc.Block())

        def js(u):
            return slice(PPU * u, PPU * u + PPU)

        def half(h):
            return slice(64 * h, 64 * h + 64)

        def grid(ap):
            return ap[:, 0:PPU * L].rearrange("p (j s) -> p j s", j=PPU)

        def quads(ap):
            return ap[:, :].rearrange("p (j r s) -> p j r s", j=PPU, r=4)

        gram_ps = [grid(bank[u]) for u in range(UNITS)]
        y2_ps = gram_ps
        y1_ps = [grid(bank[2 + u]) for u in range(UNITS)]
        dec_ps = [quads(bank[2 + u]) for u in range(UNITS)]
        ft_ps = [quads(bank[4 + u]) for u in range(UNITS)]
        conv_ps = [bank[4 + u][:, :] for u in range(UNITS)]
        b_ps = [quads(bank[6 + u]) for u in range(UNITS)]
        gn_ps = [bank[6 + u][:, 0:4 * PPU] for u in range(UNITS)]
        mask_ps = bank[7][:, 4 * PPU:4 * PPU + L]

        @block.sync
        def _(sp):
            xv = x.rearrange("(j h) c s -> (h c) j s", h=2)
            for u in range(UNITS):
                for h in range(2):
                    sp.dma_start(x_sb[half(h), js(u), :], xv[half(h), js(u), :]).then_inc(x_in[u], 16)
            sp.dma_start(k_sb[:, C_FUSE1:C_SHIFT], const[:, C_FUSE1:C_SHIFT]).then_inc(fuse_in, 16)
            ov = out.rearrange("(j h) c s -> (h c) j s", h=2)
            for u in range(UNITS):
                sp.wait_ge(out_ready, u + 1)
                for h in range(2):
                    sp.dma_start(ov[half(h), js(u), :], o_sb[half(h), js(u), :]).then_inc(stored[u], 16)
            for u in range(UNITS):
                sp.wait_ge(stored[u], 32)

        @block.gpsimd
        def _(pool):
            steps = 0

            def link(i):
                nonlocal steps
                i.then_inc(pool_step, 1)
                steps += 1
                pool.wait_ge(pool_step, steps)

            for t in (fd, ypad, ext, ppad, x2):
                pool.memset(t[:], 0.0).then_inc(pads_zero, 1)
            pool.memset(ones[:, :], 1.0).then_inc(ones_set, 1)
            link(pool.memset(mpad[:], 0.0))
            pool.wait_ge(mask_in, 16)
            m = mask_sb[:, :].rearrange("p (a r b s) -> p a r b s", a=G, r=4, b=G)
            for s in range(2):
                link(pool.tensor_tensor(mrow[:, :, :, s], m[:, :, 0, :, s], m[:, :, 1, :, s], ALU.add))
            link(pool.tensor_tensor(mcell[:], mrow[:, :, :, 0], mrow[:, :, :, 1], ALU.add))
            link(pool.tensor_scalar(mcell[:], mcell[:], 0.25, ROUND, ALU.mult, ALU.add))
            link(pool.tensor_scalar(mpad[:, 1:G + 1, 1:G + 1], mcell[:], ROUND, 1.0, ALU.subtract, ALU.mult))
            link(pool.tensor_tensor(mh1[:], mpad[:, :, 0:G], mpad[:, :, 1:G + 1], ALU.add))
            link(pool.tensor_tensor(mh2[:], mh1[:], mpad[:, :, 2:G + 2], ALU.add))
            link(pool.tensor_tensor(mv1[:], mh2[:, 0:G, :], mh2[:, 1:G + 1, :], ALU.add))
            link(pool.tensor_tensor(mv2[:], mv1[:], mh2[:, 2:G + 2, :], ALU.add))
            pool.tensor_scalar(mm10[:, :].rearrange("p (a b) -> p a b", a=G), mv2[:], 0.0, SCALE,
                               ALU.is_equal, ALU.mult).then_inc(mask_row, 1)

        @block.scalar
        def _(act):
            act.preload_act_table_set("natural_log_exp_and_others")
            act.dma_start(k_sb[:, 0:C_FUSE1], const[:, 0:C_FUSE1]).then_inc(gnk_in, 16)
            act.dma_start(mask_sb[:, :], mask).then_inc(mask_in, 16)
            for g in range(P // OC):
                act.dma_start(w_sb[OC * g:OC * g + OC, :, :], weight).then_inc(w_in, 16)
            for h in range(2):
                act.dma_start(ab_sb[half(h), :, :], ab).then_inc(ab_in, 16)
                act.dma_start(bias_sb[half(h), :], bias).then_inc(bias_in, 16)
            act.dma_start(k_sb[:, C_SHIFT:C_COLS], const[:, C_SHIFT:C_COLS]).then_inc(shift_in, 16)

            steps = 0

            def link(i):
                nonlocal steps
                i.then_inc(act_step, 1)
                steps += 1
                act.wait_ge(act_step, steps)

            def gn_seed(g, u):
                act.wait_ge(var_ready, UNITS * g + u + 1)
                link(act.activation(ln[:, g, js(u)], var[:, g, js(u)], ACT.Ln))
                act.activation(y0[:, g, js(u)], ln[:, g, js(u)], ACT.Exp, scale=-0.5).then_inc(gn_y0, 1)

            for u in range(UNITS):
                gn_seed(0, u)
            act.wait_ge(w_in, 16 * P // OC)
            act.wait_ge(ab_in, 32)
            for r in range(R):
                i = act.activation(wexp[:, r, :], w_sb[:, :, :].rearrange("p k o -> p (k o)"), ACT.Exp,
                                   scale=ab_sb[:, 1, r:r + 1])
            i.then_inc(wexp_ready, 1)
            for u in range(UNITS):
                act.wait_ge(n2_ready, u + 1)
                link(act.activation(nln[:, js(u)], n2c[:, js(u)], ACT.Ln))
                act.activation(ny0[:, js(u)], nln[:, js(u)], ACT.Exp, scale=-0.5).then_inc(norm_y0, 1)
            for u in range(UNITS):
                act.wait_ge(ft_done, u + 1)
                act.activation(ft_sb[:, js(u), :, :], ft_ps[u], ACT.Copy).then_inc(ft_ready, 1)
            act.wait_ge(pads_zero, 5)
            for u in range(UNITS):
                act.wait_ge(y1_done, u + 1)
                act.activation(ext[:, js(u), G:G + L], y1_ps[u], ACT.Copy)
                act.activation(ext[:, js(u), 1:G], y1_ps[u][:, :, L - G:L - 1], ACT.Copy)
                act.activation(ext[:, js(u), G + L:G + L + G - 1], y1_ps[u][:, :, 1:G],
                               ACT.Copy).then_inc(ext_ready, 1)
            for u in range(UNITS):
                act.wait_ge(z_ready, u + 1)
                for j in range(PPU * u, PPU * u + PPU):
                    i = act.activation(e_sb[:, j, :], z[:, j, :], ACT.Exp, bias=nmax[:, j:j + 1],
                                       accum_out=esum[:, j:j + 1])
                i.then_inc(e_ready, 1)
            for u in range(UNITS):
                act.wait_ge(b_done, u + 1)
                act.activation(b_sb[:, js(u), :, :], b_ps[u], ACT.Copy).then_inc(b_ready, 1)
            for u in range(UNITS):
                gn_seed(1, u)

        @block.tensor
        def _(te):
            def gn_groups(g, u):
                te.wait_ge(moments, UNITS * g + u + 1)
                m = mv[:, g, js(u), :].rearrange("p j m -> p (j m)")
                te.matmul(gn_ps[u][:, 0:2 * PPU], k_sb[:, C_AVG:C_AVG + P], m, start=True, stop=True)
                te.matmul(gn_ps[u][:, 2 * PPU:4 * PPU], k_sb[:, C_DIFF:C_DIFF + P], m,
                          start=True, stop=True).then_inc(groups, 1)

            te.wait_ge(gnk_in, 16)
            for u in range(UNITS):
                gn_groups(0, u)
            for u in range(UNITS):
                te.wait_ge(fd_ready, u + 1)
                for j in range(PPU):
                    for k in range(TAPS):
                        for h in range(2):
                            win = fd[half(h), PPU * u + j, k % 3, k // 3:k // 3 + G, :]
                            i = te.matmul(gram_ps[u][half(h), j, :], win, win, start=k == 0, stop=k == TAPS - 1)
                i.then_inc(gram_done, 1)
            te.wait_ge(shift_in, 16)
            for u in range(UNITS):
                te.wait_ge(f_ready, u + 1)
                for j in range(PPU):
                    for q in range(4):
                        for h in range(2):
                            i = te.matmul(ft_ps[u][half(h), j, q, :], f_sb[half(h), PPU * u + j, q, :],
                                          k_sb[half(h), C_EYE:C_EYE + L], start=True, stop=True)
                i.then_inc(ft_done, 1)
            te.wait_ge(ones_set, 1)
            te.wait_ge(mask_row, 1)
            te.wait_ge(var_ready, UNITS)
            te.matmul(mask_ps, ones[:, :], mm10[:, :], start=True, stop=True).then_inc(mask_bc, 1)
            te.wait_ge(fuse_in, 16)
            for u in range(UNITS):
                te.wait_ge(y_ready, u + 1)
                for d in range(3):
                    i = te.matmul(y1_ps[u], k_sb[:, C_FUSE1 + d * P:C_FUSE1 + d * P + P],
                                  ypad[:, js(u), d:d + L], start=d == 0, stop=d == 2)
                i.then_inc(y1_done, 1)
            for u in range(UNITS):
                te.wait_ge(ext_ready, u + 1)
                for j in range(PPU):
                    for d in range(3):
                        for h in range(2):
                            i = te.matmul(y2_ps[u][half(h), j, :], ext[half(h), PPU * u + j, G * d:G * d + L],
                                          k_sb[half(h), C_FUSE2 + d * L:C_FUSE2 + d * L + L],
                                          start=d == 0, stop=d == 2)
                i.then_inc(y2_done, 1)
            te.wait_ge(keep_ready, 1)
            for u in range(UNITS):
                te.wait_ge(p_ready, u + 1)
                for j in range(PPU):
                    for n, (s, t) in enumerate(SHIFTS):
                        rows = slice(0, 2) if s == 0 else slice(0, 1) if s > 0 else slice(1, 2)
                        cols = slice(0, 2) if t == 0 else slice(0, 1) if t > 0 else slice(1, 2)
                        nr, ncol = rows.stop - rows.start, cols.stop - cols.start
                        for h in range(2):
                            o = b_ps[u][half(h), j, :, :].rearrange("p (r c) s -> p r c s", r=2)[:, rows, cols, :]
                            sh = k_sb[half(h), C_SHIFT + n * L:C_SHIFT + n * L + L]
                            sh = sh.rearrange("p (r c s) -> p r c s", r=1, c=1).broadcast_to([64, nr, ncol, L])
                            i = te.matmul(o, ppad[half(h), PPU * u + j, 1 - t, 1 - s:1 - s + G, :], sh,
                                          start=n == 0, stop=n == len(SHIFTS) - 1)
                i.then_inc(b_done, 1)
            for u in range(UNITS):
                te.wait_ge(ft_ready, u + 1)
                te.wait_ge(b_ready, u + 1)
                for j in range(PPU):
                    for q in range(4):
                        for h in range(2):
                            i = te.matmul(dec_ps[u][half(h), j, q, :], ft_sb[half(h), PPU * u + j, q, :],
                                          b_sb[half(h), PPU * u + j, q, :], start=True, stop=True)
                i.then_inc(dec_done, 1)
            for u in range(UNITS):
                gn_groups(1, u)
            te.wait_ge(w_ready, 1)
            for u in range(UNITS):
                te.wait_ge(x2_ready, u + 1)
                for j in range(PPU):
                    for k in range(TAPS):
                        for h in range(2):
                            i = te.matmul(conv_ps[u][half(h), HW * j:HW * j + HW], w_full[half(h), k, :],
                                          x2[half(h), PPU * u + j, k // 3:k // 3 + H, k % 3:k % 3 + W],
                                          start=k == 0, stop=k == TAPS - 1)
                i.then_inc(conv_done, 1)

        @block.vector
        def _(dve):
            steps = 0

            def link(i):
                nonlocal steps
                i.then_inc(dve_step, 1)
                steps += 1
                dve.wait_ge(dve_step, steps)

            def gn_moments(g, u, src):
                for j in range(PPU * u, PPU * u + PPU):
                    i = dve.bn_stats(stats[:, g, j, :], src[:, j, :])
                link(i)
                for j in range(PPU * u, PPU * u + PPU):
                    i = dve.bn_aggr(mv[:, g, j, :], stats[:, g, j, :])
                i.then_inc(moments, 1)

            def gn_var(g, u):
                dve.wait_ge(groups, UNITS * g + u + 1)
                link(dve.tensor_copy(gst[:, g, u, :], gn_ps[u]))
                t = gst[:, g, u, :].rearrange("p (i j m) -> p i j m", i=2, m=2)
                link(dve.tensor_tensor(dif2[:, g, js(u)], t[:, 1, :, 0], t[:, 1, :, 0], ALU.mult))
                dve.scalar_tensor_tensor(var[:, g, js(u)], dif2[:, g, js(u)], GN_EPS, t[:, 0, :, 1],
                                         ALU.add, ALU.add).then_inc(var_ready, 1)

            def newton(dst, v, y, a, b):
                link(dve.tensor_tensor(a, y, y, ALU.mult))
                link(dve.scalar_tensor_tensor(b, a, -0.5, v, ALU.mult, ALU.mult))
                link(dve.scalar_tensor_tensor(dst, b, 1.5, y, ALU.add, ALU.mult))

            def gn_rstd(g, u):
                dve.wait_ge(gn_y0, UNITS * g + u + 1)
                newton(rstd[:, g, js(u)], var[:, g, js(u)], y0[:, g, js(u)], ya[:, g, js(u)], yb[:, g, js(u)])

            def normalise(dst, src, g, j):
                m = gst[:, g, j // PPU, 2 * (j % PPU):2 * (j % PPU) + 1]
                return dve.tensor_scalar(dst, src, m, rstd[:, g, j:j + 1], ALU.subtract, ALU.mult)

            for u in range(UNITS):
                dve.wait_ge(x_in[u], 32)
                gn_moments(0, u, x_sb)
            for u in range(UNITS):
                gn_var(0, u)
            dve.wait_ge(pads_zero, 5)
            for u in range(UNITS):
                gn_rstd(0, u)
                for j in range(PPU * u, PPU * u + PPU):
                    xj = x_sb[:, j, :].rearrange("p (a r b s) -> p a r b s", a=G, r=2, b=G)[:, :, 0, :, 0]
                    for c, (to, of) in enumerate(COLUMN_SHIFTS):
                        i = normalise(fd[:, j, c, 1:G + 1, to], xj[:, :, of], 0, j)
                i.then_inc(fd_ready, 1)
            for u in range(UNITS):
                for j in range(PPU * u, PPU * u + PPU):
                    for q in range(2):
                        i = normalise(f_sb[:, j, 2 * q:2 * q + 2, :].rearrange("p s (a b) -> p s a b", a=G),
                                      x_sb[:, j, :].rearrange("p (a r b s) -> p r s a b", a=G, r=2, b=G)[:, q], 0, j)
                i.then_inc(f_ready, 1)
            dve.wait_ge(shift_in, 16)
            for u in range(UNITS):
                dve.wait_ge(gram_done, u + 1)
                for j in range(PPU * u, PPU * u + PPU):
                    i = dve.scalar_tensor_tensor(gdiag[:, j, :], gram_ps[u][:, j - PPU * u, :], 1.0,
                                                 k_sb[:, C_EYE:C_EYE + L], ALU.mult, ALU.mult,
                                                 accum_out=n2[:, j:j + 1])
                link(i)
                dve.tensor_scalar(n2c[:, js(u)], n2[:, js(u)], MIN_NORM2, None, ALU.max).then_inc(n2_ready, 1)
            for u in range(UNITS):
                dve.wait_ge(norm_y0, u + 1)
                newton(rnorm[:, js(u)], n2c[:, js(u)], ny0[:, js(u)], nya[:, js(u)], nyb[:, js(u)])
                r = rnorm[:, js(u)].rearrange("p (j s) -> p j s", s=1).broadcast_to([P, PPU, L])
                dve.tensor_tensor(ypad[:, js(u), 1:L + 1], gram_ps[u], r, ALU.mult).then_inc(y_ready, 1)
            dve.wait_ge(mask_bc, 1)
            dve.tensor_copy(keep10[:, :], mask_ps)
            i = dve.tensor_scalar(keep4[:, :], mask_ps, 0.5 * SCALE, 0.25, ALU.is_gt, ALU.mult)
            i.then_inc(keep_ready, 1)
            dve.wait_ge(keep_ready, 1)
            dve.wait_ge(wexp_ready, 1)
            link(dve.tensor_scalar(wden[:], wexp[:], 1.0, None, ALU.add))
            link(dve.reciprocal(wrec[:], wden[:]))
            for r in range(R):
                i = dve.scalar_tensor_tensor(w_full[:, :, OC * r:OC * r + OC], w_sb[:, :, :], ab_sb[:, 0, r:r + 1],
                                             wrec[:, r, :].rearrange("p (k o) -> p k o", k=TAPS),
                                             ALU.mult, ALU.mult)
            i.then_inc(w_ready, 1)
            kb = keep10[:, :].rearrange("p (j s) -> p j s", j=1).broadcast_to([P, PPU, L])
            for u in range(UNITS):
                dve.wait_ge(y2_done, u + 1)
                link(dve.tensor_tensor(z[:, js(u), :], y2_ps[u], kb, ALU.mult))
                dve.tensor_reduce(nmax[:, js(u)], z[:, js(u), :], AX.X, ALU.max, negate=True).then_inc(z_ready, 1)
            for u in range(UNITS):
                dve.wait_ge(e_ready, u + 1)
                link(dve.reciprocal(erec[:, js(u)], esum[:, js(u)]))
                for j in range(PPU * u, PPU * u + PPU):
                    for c, (to, of) in enumerate(COLUMN_SHIFTS):
                        i = dve.scalar_tensor_tensor(
                            ppad[:, j, c, 1:G + 1, to], e_sb[:, j, :].rearrange("p (a b) -> p a b", a=G)[:, :, of],
                            erec[:, j:j + 1], keep4[:, :].rearrange("p (a b) -> p a b", a=G)[:, :, of],
                            ALU.mult, ALU.mult)
                i.then_inc(p_ready, 1)
            for u in range(UNITS):
                dve.wait_ge(dec_done, u + 1)
                for j in range(PPU * u, PPU * u + PPU):
                    for r in range(2):
                        xr = lambda t: t[:, j, :].rearrange("p (a r b s) -> p r a b s", a=G, r=2, b=G)[:, r]
                        d = dec_ps[u][:, j - PPU * u, 2 * r:2 * r + 2, :].rearrange("p s (a b) -> p a b s", a=G)
                        i = dve.tensor_tensor(xr(x1), d, xr(x_sb), ALU.add)
                link(i)
                gn_moments(1, u, x1)
            for u in range(UNITS):
                gn_var(1, u)
                gn_rstd(1, u)
                for j in range(PPU * u, PPU * u + PPU):
                    i = normalise(x2[:, j, 1:H + 1, 1:W + 1],
                                  x1[:, j, :].rearrange("p (a b) -> p a b", a=H), 1, j)
                i.then_inc(x2_ready, 1)
            dve.wait_ge(bias_in, 32)
            for u in range(UNITS):
                dve.wait_ge(conv_done, u + 1)
                dve.scalar_tensor_tensor(o_sb[:, js(u), :].rearrange("p j s -> p (j s)"), conv_ps[u], bias_sb[:, :],
                                         x1[:, js(u), :].rearrange("p j s -> p (j s)"),
                                         ALU.add, ALU.add).then_inc(out_ready, 1)


def kernel(**inputs):
    import concourse.bacc as _bacc
    from concourse.bass_utils import run_bass_kernel_spmd as _run

    f32 = {k: np.asarray(v) for k, v in inputs.items()}
    arrays = {
        "x_in_dram": f32["x"].reshape(N, C, HW),
        "mask_in_dram": f32["L0_conv_mask"][0:1, 0].reshape(1, MASK_SIDE * MASK_SIDE),
        "weight_in_dram": f32["L1_conv_weight"].transpose(1, 2, 3, 0).reshape(OC, TAPS, OC),
        "ab_in_dram": np.repeat(np.stack([f32["L1_conv_alphas"].reshape(R, R).T,
                                          f32["L1_conv_betas"].reshape(R, R).T], 1), OC, 0),
        "bias_in_dram": f32["L1_conv_bias"].reshape(C, 1),
        "const_dram": constants(),
    }
    arrays = {k: np.ascontiguousarray(v) for k, v in arrays.items()}
    nc = _bacc.Bacc("TRN2", target_bir_lowering=False, num_devices=1)
    args = [nc.dram_tensor(k, v.shape, mybir.dt.float32, kind="ExternalInput").ap() for k, v in arrays.items()]
    out = nc.dram_tensor("out_dram", (N, C, HW), mybir.dt.float32, kind="ExternalOutput").ap()
    build(nc, *args, out)
    r = _run(nc, [arrays], core_ids=[0])
    return r.results[0]["out_dram"].reshape(N, C, H, W)
```

```python
from contextlib import ExitStack

import concourse.bass as bass
from concourse import mybir
import numpy as np

N, C, H, W = 8, 64, 16, 16
HW = H * W
UNITS = 2
IPU = 2
G = 8
L = G * G
P = 128
TAPS = 9
R = 4
OC = C // R
GN_EPS = 1e-5
SCALE = 10.0
MASK_SIDE = 32
ROUND = 1.5 * 2.0 ** 23

FILL = (6, 1, 4, 6, 10)
F_SCALE = 16.0
Y_SCALE = 16.0
P_SCALE = 256.0
W_SCALE = 256.0
X1_SCALE = F_SCALE * P_SCALE
MIN_NORM2 = (1e-4 * F_SCALE) ** 2

SHIFTS = [(0, 0), (0, 1), (0, -1), (1, 0), (-1, 0), (1, 1), (1, -1), (-1, 1), (-1, -1)]
C_AVG, C_EYE = 0, P
C32_COLS = 2 * P
K_FUSE1 = 0
K_FUSE2 = K_FUSE1 + 3 * P
K_DIAG = K_FUSE2 + 3 * P
K_SHIFT = K_DIAG + L
K16_COLS = K_SHIFT + len(SHIFTS) * P


def constants():
    c = np.zeros((P, C32_COLS), np.float32)
    k = np.zeros((P, K16_COLS), np.float16)
    for m in range(P):
        c[m, C_EYE + m] = 1
        k[m, K_DIAG + m % L] = 1
        for p in (m, m ^ 1):
            c[p, C_AVG + m] = 0.5
    turn = np.arange(L).reshape(G, G).T.reshape(L)
    for half in (0, L):
        for d in (-1, 0, 1):
            for i in range(L):
                if 0 <= i + d < L:
                    k[half + i + d, K_FUSE1 + (d + 1) * P + half + i] = 1
                    k[half + turn[i + d], K_FUSE2 + (d + 1) * P + half + turn[i]] = 1
        for n, (s, t) in enumerate(SHIFTS):
            for a in range(G):
                for b in range(G):
                    if 0 <= a - s < G and 0 <= b - t < G:
                        k[half + G * (a - s) + b - t, K_SHIFT + n * P + half + G * a + b] = 1
    return c, k


def build(nc, x, mask, weight, par, c32, k16, out):
    fp32, fp16 = mybir.dt.float32, mybir.dt.float16
    ALU = mybir.AluOpType
    ACT = mybir.ActivationFunctionType
    AX = mybir.AxisListType

    with ExitStack() as ctx:
        def sb(name, *shape, dt=fp32):
            return ctx.enter_context(nc.sbuf_tensor(name, list(shape), dt))

        def sem(name):
            return ctx.enter_context(nc.semaphore(name))

        def per_unit(name, *shape, dt=fp32):
            return [sb(f"{name}{u}", *shape, dt=dt) for u in range(UNITS)]

        xh = per_unit("xh", P, IPU, HW)
        xg = sb("xg", P, UNITS, IPU, HW)
        c_sb = sb("c_sb", P, C32_COLS)
        k_sb = sb("k_sb", P, K16_COLS, dt=fp16)
        w_sb = sb("w_sb", P, TAPS, OC)
        par_sb = sb("par_sb", P, 2 * R + 1)
        mask_sb = sb("mask_sb", 1, MASK_SIDE * MASK_SIDE)
        ones = sb("ones", 1, P)
        mrow = sb("mrow", 1, G, G, 2)
        mcell = sb("mcell", 1, G, G)
        mpad = sb("mpad", 1, G + 2, G + 2)
        mh1 = sb("mh1", 1, G + 2, G)
        mh2 = sb("mh2", 1, G + 2, G)
        mv1 = sb("mv1", 1, G, G)
        mv2 = sb("mv2", 1, G, G)
        mrow1 = sb("mrow1", 1, L)
        keep_logit = sb("keep_logit", P, L)
        keep_prob = sb("keep_prob", P, L)
        alpha = sb("alpha", P, R)
        wexp = sb("wexp", P, R, TAPS * OC)
        wden = sb("wden", P, R, TAPS * OC)
        wrec = sb("wrec", P, R, TAPS * OC)
        w32 = sb("w32", P, TAPS, C)
        wh = sb("wh", P, TAPS, P, dt=fp16)
        wl = sb("wl", P, TAPS, P, dt=fp16)

        class Norm:
            def __init__(self, name):
                self.stats = sb(name + "_stats", P, IPU, 6)
                self.mv = sb(name + "_mv", P, IPU, 2)
                self.mean = sb(name + "_mean", P, IPU)
                self.dif = sb(name + "_dif", P, IPU)
                self.dif2 = sb(name + "_dif2", P, IPU)
                self.var = sb(name + "_var", P, IPU)
                self.ln = sb(name + "_ln", P, IPU)
                self.y0 = sb(name + "_y0", P, IPU)
                self.ya = sb(name + "_ya", P, IPU)
                self.yb = sb(name + "_yb", P, IPU)
                self.rstd = sb(name + "_rstd", P, IPU)

        norm = [[Norm(f"gn{i}{u}") for u in range(UNITS)] for i in range(2)]
        xn = per_unit("xn", P, IPU, L)
        fst = per_unit("fst", P, 3, 2 * IPU, (G + 2) * G, dt=fp16)
        fmv = per_unit("fmv", P, 2 * IPU, 2, (G + 2) ** 2, dt=fp16)
        fq = per_unit("fq", P, IPU, 4, L)
        gdiag = per_unit("gdiag", P, IPU, L)
        n2, n2c, nln, ny0, nya, nyb, rnorm = (per_unit(t, P, IPU) for t in (
            "n2", "n2c", "nln", "ny0", "nya", "nyb", "rnorm"))
        y32 = per_unit("y32", P, IPU, L)
        yh = per_unit("yh", P, IPU, L + 2, dt=fp16)
        yl = per_unit("yl", P, IPU, L + 2, dt=fp16)
        eh = per_unit("eh", P, IPU, (G + 2) * G, dt=fp16)
        el = per_unit("el", P, IPU, (G + 2) * G, dt=fp16)
        z = per_unit("z", P, IPU, L)
        nmax = per_unit("nmax", P, IPU)
        e_sb = per_unit("e_sb", P, IPU, L)
        esum = per_unit("esum", P, IPU)
        erec = per_unit("erec", P, IPU)
        p32 = per_unit("p32", P, IPU, L)
        pst = per_unit("pst", P, 3, 2 * IPU, (G + 2) * G, dt=fp16)
        bh = per_unit("bh", P, IPU, 4, L, dt=fp16)
        bl = per_unit("bl", P, IPU, 4, L, dt=fp16)
        fth = per_unit("fth", P, 4, IPU, C, dt=fp16)
        ftl = per_unit("ftl", P, 4, IPU, C, dt=fp16)
        xs = sb("xs", P, UNITS, IPU, HW)
        x1 = per_unit("x1", P, IPU, HW)
        x1b = per_unit("x1b", P, IPU * HW)
        x2 = per_unit("x2", P, IPU, HW)
        x2h = per_unit("x2h", P, IPU, H + 2, W + 2, dt=fp16)
        x2l = per_unit("x2l", P, IPU, H + 2, W + 2, dt=fp16)
        o_sb = per_unit("o_sb", P, IPU * HW)
        idle = sb("idle", P, 512, dt=fp16)

        bank = [ctx.enter_context(nc.psum_tensor(f"bank{i}", [P, 512], fp32)) for i in range(8)]

        x_in = [sem(f"x_in{u}") for u in range(UNITS)]
        xg_in, c_in, eye_in, k_in, w_in, par_in, mask_in = map(sem, (
            "xg_in", "c_in", "eye_in", "k_in", "w_in", "par_in", "mask_in"))
        stored = [sem(f"stored{u}") for u in range(UNITS)]
        zeros_f, zeros_y, zeros_p, zeros_x2, zeros_w, ones_set = map(sem, (
            "zeros_f", "zeros_y", "zeros_p", "zeros_x2", "zeros_w", "ones_set"))
        idle_set = sem("idle_set")
        pool_step, dve_step, act_step = map(sem, ("pool_step", "dve_step", "act_step"))
        mask_row, mask_bc, keep_ready = map(sem, ("mask_row", "mask_bc", "keep_ready"))
        wexp_ready, w32_ready, wh_ready, wl_ready = map(sem, ("wexp_ready", "w32_ready", "wh_ready", "wl_ready"))
        moments, groups, var_ready, mean_ready, gn_y0 = map(sem, (
            "moments", "groups", "var_ready", "mean_ready", "gn_y0"))
        xn_ready, fh_center, fl_center, fst_ready, fmv_ready, fq_ready = map(sem, (
            "xn_ready", "fh_center", "fl_center", "fst_ready", "fmv_ready", "fq_ready"))
        gram_done, n2_ready, norm_y0, y32_ready, yh_ready, yl_ready = map(sem, (
            "gram_done", "n2_ready", "norm_y0", "y32_ready", "yh_ready", "yl_ready"))
        y1_done, eh_ready, el_ready, y2_done, z_ready, e_ready = map(sem, (
            "y1_done", "eh_ready", "el_ready", "y2_done", "z_ready", "e_ready"))
        p32_ready, ph_center, pl_center, pst_ready = map(sem, ("p32_ready", "ph_center", "pl_center", "pst_ready"))
        ft_done, fth_ready, ftl_ready, b_done, bh_ready, bl_ready = map(sem, (
            "ft_done", "fth_ready", "ftl_ready", "b_done", "bh_ready", "bl_ready"))
        xs_ready, dec_done, x1_ready, x1b_ready = map(sem, ("xs_ready", "dec_done", "x1_ready", "x1b_ready"))
        x2_ready, x2h_ready, x2l_ready, conv_done, out_ready = map(sem, (
            "x2_ready", "x2h_ready", "x2l_ready", "conv_done", "out_ready"))
        block = ctx.enter_context(nc.Block())

        def half(i):
            return slice(64 * i, 64 * i + 64)

        def rows(ap):
            return ap.rearrange("p i (a b) -> p i a b", b=G)

        def flat(t):
            letters = "abcd"[:len(t.shape) - 1]
            return t[:] if len(letters) == 1 else t[:].rearrange(
                f"p {' '.join(letters)} -> p ({' '.join(letters)})")

        def inner(ap):
            side = G + 2
            return ap.rearrange("p i (a b) -> p i a b", b=side)[:, :, 1:side - 1, 1:side - 1]

        u2 = range(UNITS)
        gram_ps = [bank[u][:, 0:IPU * L].rearrange("p (i s) -> p i s", i=IPU) for u in u2]
        y2_ps = gram_ps
        y1_ps = [bank[2 + u][:, 0:IPU * (G + 2) * G].rearrange("p (i s) -> p i s", i=IPU) for u in u2]
        dec_ps = [bank[2 + u][:, :].rearrange("p (i q s) -> p i q s", i=IPU, q=4) for u in u2]
        ft_ps = [bank[4 + u][:, :].rearrange("p (q i c) -> p q i c", q=4, i=IPU) for u in u2]
        conv_ps = [bank[4 + u][:, :] for u in u2]
        b_ps = [bank[6 + u][:, :].rearrange("p (i q s) -> p i q s", i=IPU, q=4) for u in u2]
        gn_ps = [bank[6 + u][:, 0:2 * IPU] for u in u2]
        mask_ps = bank[7][:, 4 * IPU:4 * IPU + L]

        @block.sync
        def _(sp):
            xv = x.rearrange("(g u h) c s -> u (h c) g s", u=UNITS, g=2)
            sp.dma_start(xh[0][:, :, :], xv[0]).then_inc(x_in[0], 16)
            sp.dma_start(w_sb[:, :, :], weight).then_inc(w_in, 16)
            sp.dma_start(k_sb[:, :], k16).then_inc(k_in, 16)
            sp.dma_start(c_sb[:, C_EYE:C32_COLS], c32[:, C_EYE:C32_COLS]).then_inc(eye_in, 16)
            xv = x.rearrange("(g i) c s -> g c i s", g=2)
            for g in range(2):
                sp.dma_start(xg[half(g), :, :, :].rearrange("p u h s -> p (u h) s"), xv[g]).then_inc(xg_in, 16)
            ov = out.rearrange("(g u h) c s -> u h g c s", u=UNITS, g=2)
            for u in u2:
                for h in range(IPU):
                    sp.wait_ge(out_ready, IPU * u + h + 1)
                    sp.dma_start(ov[u, h], o_sb[u][:, HW * h:HW * h + HW]).then_inc(stored[u], 16)
            for u in u2:
                sp.wait_ge(stored[u], 32)

        @block.gpsimd
        def _(pool):
            steps = 0

            def link(i):
                nonlocal steps
                i.then_inc(pool_step, 1)
                steps += 1
                pool.wait_ge(pool_step, steps)

            pool.memset(idle[:, :].bitcast(fp32), 0.0).then_inc(idle_set, 1)
            pool.memset(ones[:, :], 1.0).then_inc(ones_set, 1)
            link(pool.memset(mpad[:], 0.0))
            pool.wait_ge(mask_in, 16)
            m = mask_sb[:, :].rearrange("p (a r b s) -> p a r b s", a=G, r=4, b=G)
            for s in range(2):
                link(pool.tensor_tensor(mrow[:, :, :, s], m[:, :, 0, :, s], m[:, :, 1, :, s], ALU.add))
            link(pool.tensor_tensor(mcell[:], mrow[:, :, :, 0], mrow[:, :, :, 1], ALU.add))
            link(pool.tensor_scalar(mcell[:], mcell[:], 0.25, ROUND, ALU.mult, ALU.add))
            link(pool.tensor_scalar(mpad[:, 1:G + 1, 1:G + 1], mcell[:], ROUND, 1.0, ALU.subtract, ALU.mult))
            link(pool.tensor_tensor(mh1[:], mpad[:, :, 0:G], mpad[:, :, 1:G + 1], ALU.add))
            link(pool.tensor_tensor(mh2[:], mh1[:], mpad[:, :, 2:G + 2], ALU.add))
            link(pool.tensor_tensor(mv1[:], mh2[:, 0:G, :], mh2[:, 1:G + 1, :], ALU.add))
            link(pool.tensor_tensor(mv2[:], mv1[:], mh2[:, 2:G + 2, :], ALU.add))
            pool.tensor_scalar(mrow1[:, :].rearrange("p (a b) -> p a b", a=G), mv2[:], 0.0, 1.0,
                               ALU.is_equal, ALU.mult).then_inc(mask_row, 1)
            for tiles, done in (([wh, wl], zeros_w), (yh + yl + eh + el, zeros_y), (pst, zeros_p),
                                (x2h + x2l, zeros_x2)):
                for t in tiles:
                    pool.memset(flat(t).bitcast(fp32), 0.0).then_inc(done, 1)
            pool.wait_ge(wh_ready, 1)
            pool.wait_ge(zeros_w, 2)
            pool.wait_ge(zeros_x2, 2 * UNITS)
            for g in range(2):
                i = pool.tensor_tensor(wl[half(g), :, half(g)], w32[half(g), :, :], wh[half(g), :, half(g)],
                                       ALU.subtract)
            i.then_inc(wl_ready, 1)

        @block.scalar
        def _(act):
            act.preload_act_table_set("natural_log_exp_and_others")
            xv = x.rearrange("(g u h) c s -> u (h c) g s", u=UNITS, g=2)
            act.dma_start(c_sb[:, 0:C_EYE], c32[:, 0:C_EYE]).then_inc(c_in, 16)
            act.dma_start(xh[1][:, :, :], xv[1]).then_inc(x_in[1], 16)
            act.dma_start(mask_sb[:, :], mask).then_inc(mask_in, 16)
            act.dma_start(par_sb[:, :], par).then_inc(par_in, 16)

            steps = 0

            def link(i):
                nonlocal steps
                i.then_inc(act_step, 1)
                steps += 1
                act.wait_ge(act_step, steps)

            def seed(y, v, scratch, scale):
                link(act.activation(scratch[:, :], v[:, :], ACT.Ln, scale=1.0 / scale ** 2))
                return act.activation(y[:, :], scratch[:, :], ACT.Exp, scale=-0.5)

            def gn_seed(i, u):
                n = norm[i][u]
                act.wait_ge(var_ready, UNITS * i + u + 1)
                seed(n.y0, n.var, n.ln, F_SCALE).then_inc(gn_y0, 1)

            act.wait_ge(zeros_f, 2 * UNITS)
            for u in u2:
                gn_seed(0, u)
                act.wait_ge(w_in, 16)
                act.wait_ge(par_in, 16)
                for b in range(2 * u, 2 * u + 2):
                    act.activation(wexp[:, b, :], w_sb[:, :, :].rearrange("p k o -> p (k o)"), ACT.Exp,
                                   scale=par_sb[:, R + b:R + b + 1]).then_inc(wexp_ready, 1)
                act.wait_ge(xn_ready, u + 1)
                act.activation(fst[u][:, 1, 0:IPU, G:G + L], xn[u][:, :, :], ACT.Copy).then_inc(fh_center, 1)
                act.wait_ge(fl_center, u + 1)
                c = rows(fst[u][:, 1, :, G:G + L])
                act.activation(rows(fst[u][:, 0, :, G:G + L])[:, :, :, 1:G], c[:, :, :, 0:G - 1], ACT.Copy)                   .then_inc(fst_ready, 1)
                act.activation(inner(fmv[u][half(1), :, 1, :]), c[half(1)], ACT.Copy).then_inc(fmv_ready, 1)
            act.wait_ge(xg_in, 32)
            act.activation(xs[:], xg[:], ACT.Copy, scale=X1_SCALE).then_inc(xs_ready, 1)
            act.wait_ge(zeros_y, 4 * UNITS)
            for u in u2:
                act.wait_ge(n2_ready, u + 1)
                seed(ny0[u], n2c[u], nln[u], Y_SCALE / F_SCALE).then_inc(norm_y0, 1)
                act.wait_ge(y32_ready, u + 1)
                act.activation(yh[u][:, :, 1:L + 1], y32[u][:, :, :], ACT.Copy).then_inc(yh_ready, 1)
            for u in u2:
                act.wait_ge(y1_done, u + 1)
                act.activation(eh[u][:, :, 1:(G + 2) * G - 1], y1_ps[u][:, :, 1:(G + 2) * G - 1],
                               ACT.Copy).then_inc(eh_ready, 1)
            for u in u2:
                act.wait_ge(z_ready, u + 1)
                for i in range(IPU):
                    a = act.activation(e_sb[u][:, i, :], z[u][:, i, :], ACT.Exp, bias=nmax[u][:, i:i + 1],
                                       accum_out=esum[u][:, i:i + 1])
                a.then_inc(e_ready, 1)
            act.wait_ge(zeros_p, UNITS)
            for u in u2:
                act.wait_ge(p32_ready, u + 1)
                act.activation(pst[u][:, 1, 0:IPU, G:G + L], p32[u][:, :, :], ACT.Copy).then_inc(ph_center, 1)
                act.wait_ge(pl_center, u + 1)
                c = rows(pst[u][:, 1, :, G:G + L])
                act.activation(rows(pst[u][:, 0, :, G:G + L])[:, :, :, 1:G], c[:, :, :, 0:G - 1], ACT.Copy)                   .then_inc(pst_ready, 1)
            for u in u2:
                act.wait_ge(ft_done, u + 1)
                act.activation(fth[u][:], ft_ps[u], ACT.Copy).then_inc(fth_ready, 1)
            for u in u2:
                act.wait_ge(b_done, u + 1)
                act.activation(bh[u][:], b_ps[u], ACT.Copy).then_inc(bh_ready, 1)
            act.wait_ge(w32_ready, 1)
            act.wait_ge(zeros_w, 2)
            for g in range(2):
                a = act.activation(wh[half(g), :, half(g)], w32[half(g), :, :], ACT.Copy)
            a.then_inc(wh_ready, 1)
            act.wait_ge(zeros_x2, 2 * UNITS)
            for u in u2:
                gn_seed(1, u)
                for j in range(IPU):
                    act.wait_ge(x2_ready, IPU * u + j + 1)
                    act.activation(x2h[u][:, j, 1:H + 1, 1:W + 1], x2[u][:, j, :].rearrange("p (a b) -> p a b", a=H),
                                   ACT.Copy).then_inc(x2h_ready, 1)
            for u in u2:
                act.wait_ge(x1_ready, u + 1)
                act.activation(x1b[u][:, :], x1[u][:, :, :].rearrange("p i s -> p (i s)"), ACT.Identity,
                               bias=par_sb[:, 2 * R:2 * R + 1], scale=1.0 / X1_SCALE).then_inc(x1b_ready, 1)

        @block.tensor
        def _(te):
            def gn_groups(i, u):
                te.wait_ge(moments, UNITS * i + u + 1)
                m = norm[i][u].mv[:, :, :].rearrange("p i m -> p (i m)")
                te.matmul(gn_ps[u], c_sb[:, C_AVG:C_AVG + P], m, start=True, stop=True).then_inc(groups, 1)

            def keep_clock(n, ps):
                for _ in range(n):
                    te.matmul(ps, idle[:, 0:P], idle[:, :], start=True, stop=True)

            te.wait_ge(idle_set, 1)
            keep_clock(FILL[0], bank[4][:, :])
            te.wait_ge(c_in, 16)
            gn_groups(0, 0)
            keep_clock(FILL[1], bank[4][:, :])
            gn_groups(0, 1)
            keep_clock(FILL[2], bank[4][:, :])
            for u in u2:
                te.wait_ge(fst_ready, 2 * u + 2)
                te.wait_ge(fmv_ready, 2 * u + 2)
                n = 0
                for part_st, part_mv in ((0, 0), (0, 1), (1, 0)):
                    for k in range(TAPS):
                        for g in range(2):
                            st = fst[u][:, k % 3, IPU * part_st + g, G * (k // 3):G * (k // 3) + L]
                            mv = fmv[u][:, IPU * part_mv + g, :, :].rearrange("p h (a b) -> p h a b", b=G + 2)
                            i = te.matmul(gram_ps[u][half(g), :, :], st,
                                          mv[:, :, k // 3:k // 3 + G, k % 3:k % 3 + G],
                                          start=n == 0, stop=n == 3 * TAPS - 1)
                        n += 1
                i.then_inc(gram_done, 1)
            te.wait_ge(ones_set, 1)
            te.wait_ge(mask_row, 1)
            te.wait_ge(mean_ready, UNITS)
            te.matmul(mask_ps, ones[:, :], mrow1[:, :], start=True, stop=True).then_inc(mask_bc, 1)

            def transpose_f(u):
                te.wait_ge(fq_ready, u + 1)
                for q in range(4):
                    for g in range(2):
                        i = te.matmul(ft_ps[u][half(g), q, :, :], fq[u][:, g, q, :],
                                      c_sb[:, C_EYE:C_EYE + P], start=True, stop=True)
                i.then_inc(ft_done, 1)

            te.wait_ge(eye_in, 16)
            transpose_f(0)
            te.wait_ge(k_in, 16)
            for u in u2:
                for part, ready, y in ((0, yh_ready, yh[u]), (1, yl_ready, yl[u])):
                    te.wait_ge(ready, u + 1)
                    for d in range(3):
                        first, last = part == d == 0, part == 1 and d == 2
                        m = k_sb[:, K_FUSE1 + d * P:K_FUSE1 + d * P + P]
                        te.matmul(y1_ps[u][:, :, G:G + L], m, y[:, :, d:d + L], start=first, stop=last,
                                  skip_group_check=True)
                        te.matmul(y1_ps[u][:, :, 1:G], m, y[:, :, d + L - G:d + L - 1], start=False, stop=last,
                                  skip_group_check=True)
                        i = te.matmul(y1_ps[u][:, :, G + L:2 * G + L - 1], m, y[:, :, d + 1:d + G],
                                      start=False, stop=last, skip_group_check=True)
                i.then_inc(y1_done, 1)
            for u in u2:
                for part, ready, e in ((0, eh_ready, eh[u]), (1, el_ready, el[u])):
                    te.wait_ge(ready, u + 1)
                    for d in range(3):
                        for h in range(2):
                            i = te.matmul(y2_ps[u][half(h), :, :], e[:, h, G * d:G * d + L],
                                          k_sb[:, K_FUSE2 + d * P:K_FUSE2 + d * P + P],
                                          start=part == d == 0, stop=part == 1 and d == 2)
                i.then_inc(y2_done, 1)
            transpose_f(1)
            keep_clock(FILL[3], bank[6][:, :])
            te.wait_ge(keep_ready, 1)
            for u in u2:
                te.wait_ge(pst_ready, 2 * u + 2)
                for part in range(2):
                    for n, (s, t) in enumerate(SHIFTS):
                        r0, nr = (0, 2) if s == 0 else (0, 1) if s > 0 else (1, 1)
                        c0, ncol = (0, 2) if t == 0 else (0, 1) if t > 0 else (1, 1)
                        nq = nr * ncol
                        step = 2 if ncol == 1 else 1
                        q0 = 2 * r0 + c0
                        sh = k_sb[:, K_SHIFT + n * P:K_SHIFT + n * P + P]
                        sh = sh.rearrange("p (i q s) -> p i q s", i=2, q=1).broadcast_to([P, IPU, nq, L])
                        for g in range(2):
                            i = te.matmul(b_ps[u][half(g), :, q0:q0 + step * (nq - 1) + 1:step, :],
                                          pst[u][:, 1 - t, IPU * part + g, G * (1 - s):G * (1 - s) + L], sh,
                                          start=part == n == 0, stop=part == 1 and n == len(SHIFTS) - 1)
                i.then_inc(b_done, 1)
            for u in u2:
                te.wait_ge(fth_ready, u + 1)
                te.wait_ge(ftl_ready, u + 1)
                te.wait_ge(bh_ready, u + 1)
                te.wait_ge(bl_ready, u + 1)
                for h in range(2):
                    for q in range(4):
                        for n, (ft, b) in enumerate(((fth[u], bh[u]), (ftl[u], bh[u]), (fth[u], bl[u]))):
                            for g in range(2):
                                i = te.matmul(dec_ps[u][half(g), h, q, :], ft[half(g), q, h, :], b[half(g), h, q, :],
                                              start=n == 0, stop=n == 2)
                i.then_inc(dec_done, 1)
            gn_groups(1, 0)
            keep_clock(FILL[4], conv_ps[0])
            te.wait_ge(wh_ready, 1)
            te.wait_ge(wl_ready, 1)
            for u in u2:
                te.wait_ge(x2h_ready, IPU * (u + 1))
                for n, (w, t) in enumerate(((wh, x2h[u]), (wl, x2h[u]), (wh, x2l[u]))):
                    if u == 0 and n == 1:
                        gn_groups(1, 1)
                    if n == 2:
                        te.wait_ge(x2l_ready, u + 1)
                    for k in range(TAPS):
                        i = te.matmul(conv_ps[u], w[:, k, :], t[:, :, k // 3:k // 3 + H, k % 3:k % 3 + W],
                                      start=n == k == 0, stop=n == 2 and k == TAPS - 1)
                i.then_inc(conv_done, 1)

        @block.vector
        def _(dve):
            steps = 0

            def link(i):
                nonlocal steps
                i.then_inc(dve_step, 1)
                steps += 1
                dve.wait_ge(dve_step, steps)

            def gn_moments(i, u, src):
                n = norm[i][u]
                for j in range(IPU):
                    a = dve.bn_stats(n.stats[:, j, :], src[:, j, :])
                link(a)
                for j in range(IPU):
                    a = dve.bn_aggr(n.mv[:, j, :], n.stats[:, j, :])
                a.then_inc(moments, 1)

            def gn_var(i, u, eps):
                n = norm[i][u]
                dve.wait_ge(groups, UNITS * i + u + 1)
                g = gn_ps[u].rearrange("p (i m) -> p i m", m=2)
                link(dve.tensor_tensor(n.dif[:, :], g[:, :, 0], n.mv[:, :, 0], ALU.subtract))
                link(dve.tensor_tensor(n.dif2[:, :], n.dif[:, :], n.dif[:, :], ALU.mult))
                dve.scalar_tensor_tensor(n.var[:, :], n.dif2[:, :], eps, g[:, :, 1],
                                         ALU.add, ALU.add).then_inc(var_ready, 1)
                dve.tensor_copy(n.mean[:, :], g[:, :, 0]).then_inc(mean_ready, 1)
                dve.wait_ge(mean_ready, UNITS * i + u + 1)

            def newton(dst, v, y, a, b, scale):
                link(dve.tensor_tensor(a[:, :], y[:, :], y[:, :], ALU.mult))
                link(dve.scalar_tensor_tensor(b[:, :], a[:, :], -0.5 / scale ** 2, v[:, :], ALU.mult, ALU.mult))
                link(dve.scalar_tensor_tensor(dst[:, :], b[:, :], 1.5, y[:, :], ALU.add, ALU.mult))

            def gn_rstd(i, u):
                n = norm[i][u]
                dve.wait_ge(gn_y0, UNITS * i + u + 1)
                newton(n.rstd, n.var, n.y0, n.ya, n.yb, F_SCALE)

            def normalise(dst, src, n, j):
                return dve.tensor_scalar(dst, src, n.mean[:, j:j + 1], n.rstd[:, j:j + 1], ALU.subtract, ALU.mult)

            for t in fst + fmv:
                dve.memset(flat(t).bitcast(fp32), 0.0).then_inc(zeros_f, 1)
            for u in u2:
                dve.wait_ge(x_in[u], 16)
                gn_moments(0, u, xh[u])
            dve.wait_ge(zeros_f, 2 * UNITS)
            for u in u2:
                gn_var(0, u, GN_EPS)
                gn_rstd(0, u)
                for j in range(IPU):
                    even = xh[u][:, j, :].rearrange("p (a r b s) -> p a r b s", a=G, r=2, b=G)[:, :, 0, :, 0]
                    i = normalise(xn[u][:, j, :].rearrange("p (a b) -> p a b", a=G), even, norm[0][u], j)
                i.then_inc(xn_ready, 1)
                dve.wait_ge(fh_center, u + 1)
                i = dve.tensor_tensor(fst[u][:, 1, IPU:2 * IPU, G:G + L], xn[u][:, :, :],
                                      fst[u][:, 1, 0:IPU, G:G + L], ALU.subtract)
                i.then_inc(fl_center, 1)
                dve.wait_ge(fl_center, u + 1)
                c = rows(fst[u][:, 1, :, G:G + L])
                dve.tensor_copy(rows(fst[u][:, 2, :, G:G + L])[:, :, :, 0:G - 1], c[:, :, :, 1:G])                   .then_inc(fst_ready, 1)
                dve.tensor_copy(inner(fmv[u][half(0), :, 0, :]), c[half(0)]).then_inc(fmv_ready, 1)
            dve.wait_ge(wexp_ready, R)
            link(dve.tensor_scalar(alpha[:, :], par_sb[:, 0:R], W_SCALE, None, ALU.mult))
            link(dve.tensor_scalar(wden[:], wexp[:], 1.0, None, ALU.add))

            def f_by_parity(u):
                for j in range(IPU):
                    for r in range(2):
                        i = normalise(fq[u][:, j, 2 * r:2 * r + 2, :].rearrange("p s (a b) -> p s a b", a=G),
                                      xh[u][:, j, :].rearrange("p (a r b s) -> p r s a b", a=G, r=2, b=G)[:, r],
                                      norm[0][u], j)
                i.then_inc(fq_ready, 1)

            dve.wait_ge(k_in, 16)
            dve.wait_ge(zeros_y, 4 * UNITS)
            for u in u2:
                dve.wait_ge(gram_done, u + 1)
                for j in range(IPU):
                    i = dve.scalar_tensor_tensor(gdiag[u][:, j, :], gram_ps[u][:, j, :], 1.0,
                                                 k_sb[:, K_DIAG:K_DIAG + L], ALU.mult, ALU.mult,
                                                 accum_out=n2[u][:, j:j + 1])
                link(i)
                dve.tensor_scalar(n2c[u][:, :], n2[u][:, :], MIN_NORM2, None, ALU.max).then_inc(n2_ready, 1)
                if u == 0:
                    f_by_parity(0)
                else:
                    dve.reciprocal(wrec[:, 1, :], wden[:, 1, :])
                dve.wait_ge(norm_y0, u + 1)
                newton(rnorm[u], n2c[u], ny0[u], nya[u], nyb[u], Y_SCALE / F_SCALE)
                r = rnorm[u][:, :].rearrange("p (i s) -> p i s", s=1).broadcast_to([P, IPU, L])
                dve.tensor_tensor(y32[u][:, :, :], gram_ps[u], r, ALU.mult).then_inc(y32_ready, 1)
                dve.wait_ge(yh_ready, u + 1)
                dve.tensor_tensor(yl[u][:, :, 1:L + 1], y32[u][:, :, :], yh[u][:, :, 1:L + 1],
                                  ALU.subtract).then_inc(yl_ready, 1)
                if u == 0:
                    f_by_parity(1)
                    dve.reciprocal(wrec[:, 0, :], wden[:, 0, :])
            dve.wait_ge(mask_bc, 1)
            dve.tensor_scalar(keep_logit[:, :], mask_ps, SCALE / Y_SCALE, None, ALU.mult)
            dve.tensor_scalar(keep_prob[:, :], mask_ps, P_SCALE / 4, None, ALU.mult).then_inc(keep_ready, 1)
            dve.wait_ge(keep_ready, 1)
            for u in u2:
                dve.wait_ge(eh_ready, u + 1)
                inside = slice(1, (G + 2) * G - 1)
                dve.tensor_tensor(el[u][:, :, inside], y1_ps[u][:, :, inside], eh[u][:, :, inside],
                                  ALU.subtract).then_inc(el_ready, 1)
            kb = keep_logit[:, :].rearrange("p (i s) -> p i s", i=1).broadcast_to([P, IPU, L])
            for u in u2:
                dve.wait_ge(y2_done, u + 1)
                link(dve.tensor_tensor(z[u][:, :, :], y2_ps[u], kb, ALU.mult))
                dve.tensor_reduce(nmax[u][:, :], z[u][:, :, :], AX.X, ALU.max, negate=True).then_inc(z_ready, 1)
            dve.wait_ge(zeros_p, UNITS)
            for u in u2:
                dve.wait_ge(e_ready, u + 1)
                link(dve.reciprocal(erec[u][:, :], esum[u][:, :]))
                for j in range(IPU):
                    i = dve.scalar_tensor_tensor(p32[u][:, j, :], e_sb[u][:, j, :], erec[u][:, j:j + 1],
                                                 keep_prob[:, :], ALU.mult, ALU.mult)
                i.then_inc(p32_ready, 1)
                dve.wait_ge(ph_center, u + 1)
                i = dve.tensor_tensor(pst[u][:, 1, IPU:2 * IPU, G:G + L], p32[u][:, :, :],
                                      pst[u][:, 1, 0:IPU, G:G + L], ALU.subtract)
                i.then_inc(pl_center, 1)
                dve.wait_ge(pl_center, u + 1)
                c = rows(pst[u][:, 1, :, G:G + L])
                dve.tensor_copy(rows(pst[u][:, 2, :, G:G + L])[:, :, :, 0:G - 1], c[:, :, :, 1:G])                   .then_inc(pst_ready, 1)
            for u in u2:
                dve.wait_ge(fth_ready, u + 1)
                dve.tensor_tensor(ftl[u][:], ft_ps[u], fth[u][:], ALU.subtract).then_inc(ftl_ready, 1)
            for r in range(2, R):
                i = dve.reciprocal(wrec[:, r, :], wden[:, r, :])
            link(i)
            for r in range(R):
                i = dve.scalar_tensor_tensor(w32[:, :, OC * r:OC * r + OC], w_sb[:, :, :], alpha[:, r:r + 1],
                                             wrec[:, r, :].rearrange("p (k o) -> p k o", k=TAPS),
                                             ALU.mult, ALU.mult)
            i.then_inc(w32_ready, 1)
            for u in u2:
                dve.wait_ge(bh_ready, u + 1)
                dve.tensor_tensor(bl[u][:], b_ps[u], bh[u][:], ALU.subtract).then_inc(bl_ready, 1)
            dve.wait_ge(xs_ready, 1)

            def add_attention(u):
                dve.wait_ge(dec_done, u + 1)
                for h in range(IPU):
                    for r in range(2):
                        d = dec_ps[u][:, h, 2 * r:2 * r + 2, :].rearrange("p s (a b) -> p a b s", a=G)
                        i = dve.tensor_tensor(
                            x1[u][:, h, :].rearrange("p (a r b s) -> p r a b s", a=G, r=2, b=G)[:, r], d,
                            xs[:, u, h, :].rearrange("p (a r b s) -> p r a b s", a=G, r=2, b=G)[:, r], ALU.add)
                i.then_inc(x1_ready, 1)

            def normalise_x1(u):
                gn_rstd(1, u)
                for j in range(IPU):
                    normalise(x2[u][:, j, :], x1[u][:, j, :], norm[1][u], j).then_inc(x2_ready, 1)

            def low_x2(u):
                dve.wait_ge(x2h_ready, IPU * (u + 1))
                dve.tensor_tensor(x2l[u][:, :, 1:H + 1, 1:W + 1], x2[u][:, :, :].rearrange("p i (a b) -> p i a b", a=H),
                                  x2h[u][:, :, 1:H + 1, 1:W + 1], ALU.subtract).then_inc(x2l_ready, 1)

            add_attention(0)
            dve.wait_ge(x1_ready, 1)
            gn_moments(1, 0, x1[0])
            gn_var(1, 0, GN_EPS * X1_SCALE ** 2)
            add_attention(1)
            normalise_x1(0)
            dve.wait_ge(x1_ready, 2)
            gn_moments(1, 1, x1[1])
            low_x2(0)
            gn_var(1, 1, GN_EPS * X1_SCALE ** 2)
            normalise_x1(1)
            low_x2(1)
            for u in u2:
                dve.wait_ge(conv_done, u + 1)
                dve.wait_ge(x1b_ready, u + 1)
                for h in range(IPU):
                    px = slice(HW * h, HW * h + HW)
                    dve.scalar_tensor_tensor(o_sb[u][:, px], conv_ps[u][:, px], 1.0 / (F_SCALE * W_SCALE),
                                             x1b[u][:, px], ALU.mult, ALU.add).then_inc(out_ready, 1)


def kernel(**inputs):
    import concourse.bacc as _bacc
    from concourse.bass_utils import run_bass_kernel_spmd as _run

    a = {k: np.asarray(v) for k, v in inputs.items()}
    c32, k16 = constants()
    copies = P // OC
    weight = np.tile(a["L1_conv_weight"].transpose(1, 2, 3, 0).reshape(OC, TAPS, OC), (copies, 1, 1))
    grids = [np.tile(np.repeat(a[k].reshape(R, R).T, OC, 0), (2, 1)) for k in ("L1_conv_alphas", "L1_conv_betas")]
    par = np.concatenate(grids + [np.tile(a["L1_conv_bias"].reshape(C, 1), (2, 1))], 1)
    arrays = {
        "x_in_dram": a["x"].reshape(N, C, HW),
        "mask_in_dram": a["L0_conv_mask"][0:1, 0].reshape(1, MASK_SIDE * MASK_SIDE),
        "weight_in_dram": weight,
        "par_in_dram": par,
        "c32_dram": c32,
        "k16_dram": k16,
    }
    arrays = {k: np.ascontiguousarray(v) for k, v in arrays.items()}
    nc = _bacc.Bacc("TRN2", target_bir_lowering=False, num_devices=1)
    args = [nc.dram_tensor(k, v.shape, mybir.dt.from_np(v.dtype), kind="ExternalInput").ap() for k, v in arrays.items()]
    out = nc.dram_tensor("out_dram", (N, C, HW), mybir.dt.float32, kind="ExternalOutput").ap()
    build(nc, *args, out)
    r = _run(nc, [arrays], core_ids=[0])
    return r.results[0]["out_dram"].reshape(N, C, H, W)
```

```python
from contextlib import ExitStack

import concourse.bass as bass
from concourse import mybir
import numpy as np

N, C, H, W = 8, 64, 16, 16
HW = H * W
UNITS = 2
IPU = 2
G = 8
L = G * G
P = 128
TAPS = 9
R = 4
OC = C // R
BLOCKS = R // 2
GN_EPS = 1e-5
SCALE = 10.0
MASK_SIDE = 32
ROUND = 1.5 * 2.0 ** 23

FILL = {"x": 8, "statistics": 4, "high f of unit 0": 5, "low f of unit 0": 1, "high f of unit 1": 4,
        "low f of unit 1": 3, "sums of unit 0": 2}
F_SCALE = 16.0
Y_SCALE = 16.0
P_SCALE = 256.0
W_SCALE = 256.0
X1_SCALE = F_SCALE * P_SCALE
MIN_NORM2 = (1e-4 * F_SCALE) ** 2

SHIFTS = [(0, 0), (0, 1), (0, -1), (1, 0), (-1, 0), (1, 1), (1, -1), (-1, 1), (-1, -1)]
C_AVG, C_EYE = 0, P
C32_COLS = 2 * P
K_FUSE1 = 0
K_FUSE2 = K_FUSE1 + 3 * P
K_DIAG = K_FUSE2 + 3 * P
K_SHIFT = K_DIAG + L
K16_COLS = K_SHIFT + len(SHIFTS) * P


def constants():
    c = np.zeros((P, C32_COLS), np.float32)
    k = np.zeros((P, K16_COLS), np.float16)
    for m in range(P):
        c[m, C_EYE + m] = 1
        k[m, K_DIAG + m % L] = 1
        for p in (m, m ^ 1):
            c[p, C_AVG + m] = 0.5
    turn = np.arange(L).reshape(G, G).T.reshape(L)
    for half in (0, L):
        for d in (-1, 0, 1):
            for i in range(L):
                if 0 <= i + d < L:
                    k[half + i + d, K_FUSE1 + (d + 1) * P + half + i] = 1
                    k[half + turn[i + d], K_FUSE2 + (d + 1) * P + half + turn[i]] = 1
        for n, (s, t) in enumerate(SHIFTS):
            for a in range(G):
                for b in range(G):
                    if 0 <= a - s < G and 0 <= b - t < G:
                        k[half + G * (a - s) + b - t, K_SHIFT + n * P + half + G * a + b] = 1
    return c, k


def build(nc, x, mask, weight, par, c32, k16, out):
    fp32, fp16 = mybir.dt.float32, mybir.dt.float16
    ALU = mybir.AluOpType
    ACT = mybir.ActivationFunctionType
    AX = mybir.AxisListType

    with ExitStack() as ctx:
        def sb(name, *shape, dt=fp32):
            return ctx.enter_context(nc.sbuf_tensor(name, list(shape), dt))

        def sem(name):
            return ctx.enter_context(nc.semaphore(name))

        def per_unit(name, *shape, dt=fp32):
            return [sb(f"{name}{u}", *shape, dt=dt) for u in range(UNITS)]

        xh = per_unit("xh", P, IPU, HW)
        xg = sb("xg", P, UNITS, IPU, HW)
        c_sb = sb("c_sb", P, C32_COLS)
        k_sb = sb("k_sb", P, K16_COLS, dt=fp16)
        w_sb = sb("w_sb", P, TAPS, OC)
        par_sb = sb("par_sb", P, 2 * BLOCKS + 1)
        mask_sb = sb("mask_sb", 1, MASK_SIDE * MASK_SIDE)
        ones = sb("ones", 1, P)
        mrow = sb("mrow", 1, G, G, 2)
        mcell = sb("mcell", 1, G, G)
        mpad = sb("mpad", 1, G + 2, G + 2)
        mh1 = sb("mh1", 1, G + 2, G)
        mh2 = sb("mh2", 1, G + 2, G)
        mv1 = sb("mv1", 1, G, G)
        mv2 = sb("mv2", 1, G, G)
        mrow1 = sb("mrow1", 1, L)
        keep_logit = sb("keep_logit", P, L)
        keep_prob = sb("keep_prob", P, L)
        walpha, wexp, wden, wrec = (sb(t, P, BLOCKS, TAPS * OC) for t in ("walpha", "wexp", "wden", "wrec"))
        w32 = sb("w32", P, TAPS, BLOCKS * OC)
        wh = sb("wh", P, TAPS, P, dt=fp16)
        wl = sb("wl", P, TAPS, P, dt=fp16)

        class Norm:
            def __init__(self, name):
                self.stats = sb(name + "_stats", P, IPU, 6)
                self.mv = sb(name + "_mv", P, IPU, 2)
                self.mean = sb(name + "_mean", P, IPU)
                self.dif = sb(name + "_dif", P, IPU)
                self.dif2 = sb(name + "_dif2", P, IPU)
                self.var = sb(name + "_var", P, IPU)
                self.ln = sb(name + "_ln", P, IPU)
                self.y0 = sb(name + "_y0", P, IPU)
                self.ya = sb(name + "_ya", P, IPU)
                self.yb = sb(name + "_yb", P, IPU)
                self.rstd = sb(name + "_rstd", P, IPU)

        norm = [[Norm(f"gn{i}{u}") for u in range(UNITS)] for i in range(2)]
        xn = per_unit("xn", P, IPU, L)
        fst = per_unit("fst", P, 3, 2 * IPU, (G + 2) * G, dt=fp16)
        fmv = per_unit("fmv", P, 2 * IPU, 2, (G + 2) ** 2, dt=fp16)
        fq = per_unit("fq", P, IPU, 4, L)
        gdiag = per_unit("gdiag", P, IPU, L)
        n2, n2c, nln, ny0, nya, nyb, rnorm = (per_unit(t, P, IPU) for t in (
            "n2", "n2c", "nln", "ny0", "nya", "nyb", "rnorm"))
        y32 = per_unit("y32", P, IPU, L)
        yh = per_unit("yh", P, IPU, L + 2, dt=fp16)
        yl = per_unit("yl", P, IPU, L + 2, dt=fp16)
        eh = per_unit("eh", P, IPU, (G + 2) * G, dt=fp16)
        el = per_unit("el", P, IPU, (G + 2) * G, dt=fp16)
        z = per_unit("z", P, IPU, L)
        nmax = per_unit("nmax", P, IPU)
        e_sb = per_unit("e_sb", P, IPU, L)
        esum = per_unit("esum", P, IPU)
        erec = per_unit("erec", P, IPU)
        p32 = per_unit("p32", P, IPU, L)
        pst = per_unit("pst", P, 3, 2 * IPU, (G + 2) * G, dt=fp16)
        bh = per_unit("bh", P, IPU, 4, L, dt=fp16)
        bl = per_unit("bl", P, IPU, 4, L, dt=fp16)
        fth = per_unit("fth", P, 4, IPU, C, dt=fp16)
        ftl = per_unit("ftl", P, 4, IPU, C, dt=fp16)
        eye_x1 = sb("eye_x1", P, P)
        x1 = per_unit("x1", P, IPU, HW)
        x1b = per_unit("x1b", P, IPU * HW)
        x2 = per_unit("x2", P, IPU, HW)
        x2h = per_unit("x2h", P, IPU, H + 2, W + 2, dt=fp16)
        x2l = per_unit("x2l", P, IPU, H + 2, W + 2, dt=fp16)
        o_sb = per_unit("o_sb", P, IPU * HW)
        idle = sb("idle", P, 512, dt=fp16)

        bank = [ctx.enter_context(nc.psum_tensor(f"bank{i}", [P, 512], fp32)) for i in range(8)]

        x_in = [sem(f"x_in{u}") for u in range(UNITS)]
        xg_in, c_in, eye_in, k_in, w_in, par_in, mask_in = map(sem, (
            "xg_in", "c_in", "eye_in", "k_in", "w_in", "par_in", "mask_in"))
        stored = [sem(f"stored{u}") for u in range(UNITS)]
        zeros_f, zeros_y, zeros_p, zeros_x2, zeros_w, ones_set = map(sem, (
            "zeros_f", "zeros_y", "zeros_p", "zeros_x2", "zeros_w", "ones_set"))
        idle_set = sem("idle_set")
        pool_step, dve_step, act_step = map(sem, ("pool_step", "dve_step", "act_step"))
        mask_row, mask_bc, keep_ready = map(sem, ("mask_row", "mask_bc", "keep_ready"))
        wden_ready, wrec_ready, walpha_ready = map(sem, ("wden_ready", "wrec_ready", "walpha_ready"))
        wexp_ready, w32_ready, wh_ready, wl_ready = map(sem, ("wexp_ready", "w32_ready", "wh_ready", "wl_ready"))
        moments, groups, var_ready, mean_ready, gn_y0 = map(sem, (
            "moments", "groups", "var_ready", "mean_ready", "gn_y0"))
        xn_ready, fh_center, fl_center, fq_ready = map(sem, ("xn_ready", "fh_center", "fl_center", "fq_ready"))
        f_copied = [[sem(f"f_copied{u}{part}") for part in range(2)] for u in range(UNITS)]
        gram_done, n2_ready, norm_y0, y32_ready, yh_ready, yl_ready = map(sem, (
            "gram_done", "n2_ready", "norm_y0", "y32_ready", "yh_ready", "yl_ready"))
        rnorm_ready = sem("rnorm_ready")
        y1_done, eh_ready, el_ready, y2_done, z_ready, e_ready = map(sem, (
            "y1_done", "eh_ready", "el_ready", "y2_done", "z_ready", "e_ready"))
        p32_ready, ph_center, pl_center = map(sem, ("p32_ready", "ph_center", "pl_center"))
        p_copied = [[sem(f"p_copied{u}{part}") for part in range(2)] for u in range(UNITS)]
        ft_done, fth_ready, ftl_ready, b_done, bh_ready, bl_ready = map(sem, (
            "ft_done", "fth_ready", "ftl_ready", "b_done", "bh_ready", "bl_ready"))
        eye_x1_ready, dec_done, x1_ready, x1b_ready = map(sem, ("eye_x1_ready", "dec_done", "x1_ready", "x1b_ready"))
        x2_ready, x2h_ready, x2l_ready, conv_done, out_ready = map(sem, (
            "x2_ready", "x2h_ready", "x2l_ready", "conv_done", "out_ready"))
        block = ctx.enter_context(nc.Block())

        def half(i):
            return slice(64 * i, 64 * i + 64)

        def rows(ap):
            return ap.rearrange("p i (a b) -> p i a b", b=G)

        def flat(t):
            letters = "abcd"[:len(t.shape) - 1]
            return t[:] if len(letters) == 1 else t[:].rearrange(
                f"p {' '.join(letters)} -> p ({' '.join(letters)})")

        def of(part):
            return slice(IPU * part, IPU * part + IPU)

        def inner(ap):
            side = G + 2
            return ap.rearrange("p i (a b) -> p i a b", b=side)[:, :, 1:side - 1, 1:side - 1]

        u2 = range(UNITS)
        gram_ps = [bank[u][:, 0:IPU * L].rearrange("p (i s) -> p i s", i=IPU) for u in u2]
        y2_ps = gram_ps
        y1_ps = [bank[2 + u][:, 0:IPU * (G + 2) * G].rearrange("p (i s) -> p i s", i=IPU) for u in u2]
        dec_ps = [bank[2 + u][:, :].rearrange("p (i q s) -> p i q s", i=IPU, q=4) for u in u2]
        x1_ps = [bank[2 + u][:, :].rearrange("p (i s) -> p i s", i=IPU) for u in u2]
        ft_ps = [bank[4 + u][:, :].rearrange("p (q i c) -> p q i c", q=4, i=IPU) for u in u2]
        conv_ps = bank[4][:, :]
        conv1_ps = [bank[5][:, 0:HW], bank[6][:, 0:HW]]
        b_ps = [bank[6 + u][:, :].rearrange("p (i q s) -> p i q s", i=IPU, q=4) for u in u2]
        gn_ps = [bank[6 + u][:, 0:2 * IPU] for u in u2]
        mask_ps = bank[7][:, 4 * IPU:4 * IPU + L]

        @block.sync
        def _(sp):
            xv = x.rearrange("(g u h) c s -> u (h c) g s", u=UNITS, g=2)
            sp.dma_start(xh[0][:, :, :], xv[0]).then_inc(x_in[0], 16)
            sp.dma_start(w_sb[:, :, :], weight).then_inc(w_in, 16)
            sp.dma_start(mask_sb[:, :], mask).then_inc(mask_in, 16)
            sp.dma_start(k_sb[:, :], k16).then_inc(k_in, 16)
            sp.dma_start(c_sb[:, C_EYE:C32_COLS], c32[:, C_EYE:C32_COLS]).then_inc(eye_in, 16)
            xv = x.rearrange("(g i) c s -> g c i s", g=2)
            for g in range(2):
                sp.dma_start(xg[half(g), :, :, :].rearrange("p u h s -> p (u h) s"), xv[g]).then_inc(xg_in, 16)
            ov = out.rearrange("(g u h) c s -> u h g c s", u=UNITS, g=2)
            for u in u2:
                for h in range(IPU):
                    sp.wait_ge(out_ready, IPU * u + h + 1)
                    sp.dma_start(ov[u, h], o_sb[u][:, HW * h:HW * h + HW]).then_inc(stored[u], 16)
            for u in u2:
                sp.wait_ge(stored[u], 32)

        @block.gpsimd
        def _(pool):
            steps = 0

            def link(i):
                nonlocal steps
                i.then_inc(pool_step, 1)
                steps += 1
                pool.wait_ge(pool_step, steps)

            def zero(tiles, done):
                for t in tiles:
                    pool.memset(flat(t).bitcast(fp32), 0.0).then_inc(done, 1)

            zero([idle], idle_set)
            pool.memset(ones[:, :], 1.0).then_inc(ones_set, 1)
            link(pool.memset(mpad[:], 0.0))
            zero(yh + yl + eh + el, zeros_y)
            zero(pst, zeros_p)
            zero([wh, wl], zeros_w)
            pool.wait_ge(mask_in, 16)
            m = mask_sb[:, :].rearrange("p (a r b s) -> p a r b s", a=G, r=4, b=G)
            for s in range(2):
                link(pool.tensor_tensor(mrow[:, :, :, s], m[:, :, 0, :, s], m[:, :, 1, :, s], ALU.add))
            link(pool.tensor_tensor(mcell[:], mrow[:, :, :, 0], mrow[:, :, :, 1], ALU.add))
            link(pool.tensor_scalar(mcell[:], mcell[:], 0.25, ROUND, ALU.mult, ALU.add))
            link(pool.tensor_scalar(mpad[:, 1:G + 1, 1:G + 1], mcell[:], ROUND, 1.0, ALU.subtract, ALU.mult))
            link(pool.tensor_tensor(mh1[:], mpad[:, :, 0:G], mpad[:, :, 1:G + 1], ALU.add))
            link(pool.tensor_tensor(mh2[:], mh1[:], mpad[:, :, 2:G + 2], ALU.add))
            link(pool.tensor_tensor(mv1[:], mh2[:, 0:G, :], mh2[:, 1:G + 1, :], ALU.add))
            link(pool.tensor_tensor(mv2[:], mv1[:], mh2[:, 2:G + 2, :], ALU.add))
            pool.tensor_scalar(mrow1[:, :].rearrange("p (a b) -> p a b", a=G), mv2[:], 0.0, 1.0,
                               ALU.is_equal, ALU.mult).then_inc(mask_row, 1)

            def f_by_parity(u, j):
                for q in range(2):
                    pool.tensor_scalar(
                        fq[u][:, j, 2 * q:2 * q + 2, :].rearrange("p s (a b) -> p s a b", a=G),
                        xh[u][:, j, :].rearrange("p (a r b s) -> p r s a b", a=G, r=2, b=G)[:, q],
                        norm[0][u].mean[:, j:j + 1], norm[0][u].rstd[:, j:j + 1],
                        ALU.subtract, ALU.mult).then_inc(fq_ready, 1)

            pool.wait_ge(xn_ready, 1)
            f_by_parity(0, 0)
            for b in range(BLOCKS):
                pool.wait_ge(wexp_ready, b + 1)
                pool.tensor_scalar(wden[:, b, :], wexp[:, b, :], 1.0, 1.0 / W_SCALE, ALU.add,
                                   ALU.mult).then_inc(wden_ready, 1)
            f_by_parity(0, 1)
            pool.wait_ge(xn_ready, 2)
            for j in range(IPU):
                f_by_parity(1, j)
            zero(x2h + x2l, zeros_x2)
            pool.wait_ge(walpha_ready, BLOCKS)
            for b in range(BLOCKS):
                pool.wait_ge(wrec_ready, 2 * b + 2)
                w3 = lambda t: t[:, b, :].rearrange("p (k o) -> p k o", k=TAPS)
                pool.tensor_tensor(w32[:, :, OC * b:OC * b + OC], w3(walpha), w3(wrec),
                                   ALU.mult).then_inc(w32_ready, 1)
            pool.wait_ge(wh_ready, 4)
            pool.wait_ge(zeros_w, 2)
            pool.wait_ge(zeros_x2, 2 * UNITS)
            for g in range(2):
                for src in range(2):
                    o = BLOCKS * OC * src
                    pool.tensor_tensor(wl[half(g), :, C * g + o:C * g + o + C // 2], w32[half(src), :, :],
                                       wh[half(src), :, C * src + o:C * src + o + C // 2],
                                       ALU.subtract).then_inc(wl_ready, 1)

        @block.scalar
        def _(act):
            act.preload_act_table_set("natural_log_exp_and_others")
            xv = x.rearrange("(g u h) c s -> u (h c) g s", u=UNITS, g=2)
            act.dma_start(c_sb[:, 0:C_EYE], c32[:, 0:C_EYE]).then_inc(c_in, 16)
            act.dma_start(xh[1][:, :, :], xv[1]).then_inc(x_in[1], 16)
            act.dma_start(par_sb[:, :], par).then_inc(par_in, 16)

            steps = 0

            def link(i):
                nonlocal steps
                i.then_inc(act_step, 1)
                steps += 1
                act.wait_ge(act_step, steps)

            def seed(y, v, scratch, scale):
                link(act.activation(scratch[:, :], v[:, :], ACT.Ln, scale=1.0 / scale ** 2))
                return act.activation(y[:, :], scratch[:, :], ACT.Exp, scale=-0.5)

            def gn_seed(i, u):
                n = norm[i][u]
                act.wait_ge(var_ready, UNITS * i + u + 1)
                seed(n.y0, n.var, n.ln, F_SCALE).then_inc(gn_y0, 1)

            def exp_weight(b):
                act.activation(wexp[:, b, :], w_sb[:, :, :].rearrange("p k o -> p (k o)"), ACT.Exp,
                               scale=par_sb[:, BLOCKS + b:BLOCKS + b + 1]).then_inc(wexp_ready, 1)

            def shift_right(t, part):
                return act.activation(rows(t[:, 0, of(part), G:G + L])[:, :, :, 1:G],
                                      rows(t[:, 1, of(part), G:G + L])[:, :, :, 0:G - 1], ACT.Copy)

            def copies_of_f(u, part):
                act.wait_ge((fh_center, fl_center)[part], u + 1)
                shift_right(fst[u], part).then_inc(f_copied[u][part], 1)
                act.activation(inner(fmv[u][half(1), of(part), 1, :]), rows(fst[u][half(1), 1, of(part), G:G + L]),
                               ACT.Copy).then_inc(f_copied[u][part], 1)

            def weight_alpha(b):
                act.activation(walpha[:, b, :], w_sb[:, :, :].rearrange("p k o -> p (k o)"), ACT.Copy,
                               scale=par_sb[:, b:b + 1]).then_inc(walpha_ready, 1)

            def norm_seed(u):
                act.wait_ge(n2_ready, u + 1)
                seed(ny0[u], n2c[u], nln[u], Y_SCALE / F_SCALE).then_inc(norm_y0, 1)

            def high_y1(u):
                act.wait_ge(y1_done, u + 1)
                act.activation(eh[u][:, :, 1:(G + 2) * G - 1], y1_ps[u][:, :, 1:(G + 2) * G - 1],
                               ACT.Copy).then_inc(eh_ready, 1)

            def exp_logits(u):
                act.wait_ge(z_ready, u + 1)
                for i in range(IPU):
                    a = act.activation(e_sb[u][:, i, :], z[u][:, i, :], ACT.Exp, bias=nmax[u][:, i:i + 1],
                                       accum_out=esum[u][:, i:i + 1])
                a.then_inc(e_ready, 1)

            def copies_of_p(u, part):
                act.wait_ge((ph_center, pl_center)[part], u + 1)
                shift_right(pst[u], part).then_inc(p_copied[u][part], 1)

            def high_ft(u):
                act.wait_ge(ft_done, u + 1)
                act.activation(fth[u][:], ft_ps[u], ACT.Copy).then_inc(fth_ready, 1)

            def high_b(u):
                act.wait_ge(b_done, u + 1)
                act.activation(bh[u][:], b_ps[u], ACT.Copy).then_inc(bh_ready, 1)

            def x1_and_bias(u):
                act.wait_ge(x1_ready, 2 * IPU * (u + 1))
                act.activation(x1b[u][:, :], x1[u][:, :, :].rearrange("p i s -> p (i s)"), ACT.Identity,
                               bias=par_sb[:, 2 * BLOCKS:2 * BLOCKS + 1], scale=1.0 / X1_SCALE).then_inc(x1b_ready, 1)

            act.wait_ge(zeros_f, 2 * UNITS)
            gn_seed(0, 0)
            copies_of_f(0, 0)
            copies_of_f(0, 1)
            gn_seed(0, 1)
            act.wait_ge(w_in, 16)
            act.wait_ge(par_in, 16)
            exp_weight(0)
            exp_weight(1)
            copies_of_f(1, 0)
            norm_seed(0)
            copies_of_f(1, 1)
            weight_alpha(0)
            weight_alpha(1)
            act.wait_ge(eye_in, 16)
            act.activation(eye_x1[:], c_sb[:, C_EYE:C_EYE + P], ACT.Copy, scale=X1_SCALE).then_inc(eye_x1_ready, 1)
            act.wait_ge(zeros_y, 4 * UNITS)
            high_y1(0)
            norm_seed(1)
            act.wait_ge(zeros_p, UNITS)
            exp_logits(0)
            copies_of_p(0, 0)
            copies_of_p(0, 1)
            high_y1(1)
            high_ft(0)
            high_b(0)
            exp_logits(1)
            copies_of_p(1, 0)
            high_ft(1)
            copies_of_p(1, 1)
            act.wait_ge(w32_ready, BLOCKS)
            act.wait_ge(zeros_w, 2)
            for g in range(2):
                for src in range(2):
                    o = C * g + BLOCKS * OC * src
                    act.activation(wh[half(g), :, o:o + C // 2], w32[half(src), :, :],
                                   ACT.Copy).then_inc(wh_ready, 1)
            gn_seed(1, 0)
            high_b(1)
            x1_and_bias(0)
            gn_seed(1, 1)
            x1_and_bias(1)

        @block.tensor
        def _(te):
            def gn_groups(i, u):
                te.wait_ge(moments, UNITS * i + u + 1)
                m = norm[i][u].mv[:, :, :].rearrange("p i m -> p (i m)")
                te.matmul(gn_ps[u], c_sb[:, C_AVG:C_AVG + P], m, start=True, stop=True).then_inc(groups, 1)

            def keep_clock(n, ps):
                for _ in range(n):
                    te.matmul(ps, idle[:, 0:P], idle[:, :], start=True, stop=True)

            def gram(u, parts):
                for part_st, part_mv in parts:
                    te.wait_ge(f_copied[u][max(part_st, part_mv)], 4)
                    for k in range(TAPS):
                        for g in range(2):
                            st = fst[u][:, k % 3, IPU * part_st + g, G * (k // 3):G * (k // 3) + L]
                            mv = fmv[u][:, IPU * part_mv + g, :, :].rearrange("p h (a b) -> p h a b", b=G + 2)
                            i = te.matmul(gram_ps[u][half(g), :, :], st,
                                          mv[:, :, k // 3:k // 3 + G, k % 3:k % 3 + G],
                                          start=part_st == part_mv == k == 0, stop=part_st == 1 and k == TAPS - 1)
                return i

            def transpose_f(u, parities):
                te.wait_ge(fq_ready, 2 * IPU * (u + 1))
                for q in parities:
                    for g in range(2):
                        i = te.matmul(ft_ps[u][half(g), q, :, :], fq[u][:, g, q, :],
                                      c_sb[:, C_EYE:C_EYE + P], start=True, stop=True)
                return i

            def fuse1(u, part):
                te.wait_ge((yh_ready, yl_ready)[part], u + 1)
                y = (yh, yl)[part][u]
                for d in range(3):
                    first, last = part == d == 0, part == 1 and d == 2
                    m = k_sb[:, K_FUSE1 + d * P:K_FUSE1 + d * P + P]
                    te.matmul(y1_ps[u][:, :, G:G + L], m, y[:, :, d:d + L], start=first, stop=last,
                              skip_group_check=True)
                    te.matmul(y1_ps[u][:, :, 1:G], m, y[:, :, d + L - G:d + L - 1], start=False, stop=last,
                              skip_group_check=True)
                    i = te.matmul(y1_ps[u][:, :, G + L:2 * G + L - 1], m, y[:, :, d + 1:d + G],
                                  start=False, stop=last, skip_group_check=True)
                return i

            def fuse2(u, part):
                te.wait_ge((eh_ready, el_ready)[part], u + 1)
                e = (eh, el)[part][u]
                for d in range(3):
                    for h in range(2):
                        i = te.matmul(y2_ps[u][half(h), :, :], e[:, h, G * d:G * d + L],
                                      k_sb[:, K_FUSE2 + d * P:K_FUSE2 + d * P + P],
                                      start=part == d == 0, stop=part == 1 and d == 2)
                return i

            def sum_shifts(u, part, shifts=range(len(SHIFTS))):
                te.wait_ge(p_copied[u][part], 2)
                for n in shifts:
                    s, t = SHIFTS[n]
                    r0, nr = (0, 2) if s == 0 else (0, 1) if s > 0 else (1, 1)
                    c0, ncol = (0, 2) if t == 0 else (0, 1) if t > 0 else (1, 1)
                    nq = nr * ncol
                    step = 2 if ncol == 1 else 1
                    q0 = 2 * r0 + c0
                    sh = k_sb[:, K_SHIFT + n * P:K_SHIFT + n * P + P]
                    sh = sh.rearrange("p (i q s) -> p i q s", i=2, q=1).broadcast_to([P, IPU, nq, L])
                    for g in range(2):
                        i = te.matmul(b_ps[u][half(g), :, q0:q0 + step * (nq - 1) + 1:step, :],
                                      pst[u][:, 1 - t, IPU * part + g, G * (1 - s):G * (1 - s) + L], sh,
                                      start=part == n == 0, stop=part == 1 and n == len(SHIFTS) - 1)
                return i

            def put_x(u):
                te.wait_ge(eye_x1_ready, 1)
                te.wait_ge(xg_in, 32)
                te.wait_ge(el_ready, u + 1)
                for h in range(IPU):
                    for r in range(2):
                        te.matmul(dec_ps[u][:, h, 2 * r:2 * r + 2, :], eye_x1[:],
                                  xg[:, u, h, :].rearrange("p (a r b s) -> p r s a b", a=G, r=2, b=G)[:, r],
                                  start=h == r == 0, stop=False, skip_group_check=True)

            def deconv_high(u):
                te.wait_ge(fth_ready, u + 1)
                te.wait_ge(ftl_ready, u + 1)
                te.wait_ge(bh_ready, u + 1)
                deconv_part(u, fth[u], bh[u], False)
                deconv_part(u, ftl[u], bh[u], False)

            def deconv_low(u):
                te.wait_ge(bl_ready, u + 1)
                deconv_part(u, fth[u], bl[u], True).then_inc(dec_done, 1)

            def deconv_part(u, ft, b, last):
                for h in range(2):
                    for q in range(4):
                        for g in range(2):
                            i = te.matmul(dec_ps[u][half(g), h, q, :], ft[half(g), q, h, :], b[half(g), h, q, :],
                                          start=False, stop=last, skip_group_check=True)
                return i

            def conv(part, taps=range(TAPS)):
                w, t = ((wh, x2h[0]), (wh, x2l[0]), (wl, x2h[0]))[part]
                for k in taps:
                    i = te.matmul(conv_ps, w[:, k, :], t[:, :, k // 3:k // 3 + H, k % 3:k % 3 + W],
                                  start=part == k == 0, stop=part == 2 and k == TAPS - 1)
                return i

            def conv_image(h):
                for n, (w, t) in enumerate(((wh, x2h[1]), (wh, x2l[1]), (wl, x2h[1]))):
                    if n == 0:
                        te.wait_ge(x2h_ready, IPU + h + 1)
                    if n == 1:
                        te.wait_ge(x2l_ready, 2 + h)
                    for k in range(TAPS):
                        i = te.matmul(conv1_ps[h], w[:, k, :], t[:, h, k // 3:k // 3 + H, k % 3:k % 3 + W],
                                      start=n == k == 0, stop=n == 2 and k == TAPS - 1)
                return i

            te.wait_ge(idle_set, 1)
            keep_clock(FILL["x"], bank[4][:, :])
            te.wait_ge(c_in, 16)
            gn_groups(0, 0)
            keep_clock(FILL["statistics"], bank[4][:, :])
            gn_groups(0, 1)
            keep_clock(FILL["high f of unit 0"], bank[4][:, :])
            gram(0, ((0, 0),))
            keep_clock(FILL["low f of unit 0"], bank[6][:, :])
            gram(0, ((0, 1), (1, 0))).then_inc(gram_done, 1)
            keep_clock(FILL["high f of unit 1"], bank[6][:, :])
            gram(1, ((0, 0),))
            keep_clock(FILL["low f of unit 1"], bank[6][:, :])
            gram(1, ((0, 1),))
            te.wait_ge(k_in, 16)
            fuse1(0, 0)
            fuse1(0, 1).then_inc(y1_done, 1)
            te.wait_ge(ones_set, 1)
            te.wait_ge(mask_row, 1)
            te.wait_ge(mean_ready, UNITS)
            te.matmul(mask_ps, ones[:, :], mrow1[:, :], start=True, stop=True).then_inc(mask_bc, 1)
            gram(1, ((1, 0),)).then_inc(gram_done, 1)
            fuse2(0, 0)
            fuse2(0, 1).then_inc(y2_done, 1)
            te.wait_ge(eye_in, 16)
            transpose_f(0, range(4)).then_inc(ft_done, 1)
            put_x(0)
            fuse1(1, 0)
            fuse1(1, 1).then_inc(y1_done, 1)
            transpose_f(1, range(0, 2))
            te.wait_ge(keep_ready, 1)
            sum_shifts(0, 0)
            fuse2(1, 0)
            fuse2(1, 1).then_inc(y2_done, 1)
            sum_shifts(0, 1).then_inc(b_done, 1)
            transpose_f(1, range(2, 4)).then_inc(ft_done, 1)
            keep_clock(FILL["sums of unit 0"], bank[7][:, :])
            deconv_high(0)
            deconv_low(0)
            sum_shifts(1, 0)
            gn_groups(1, 0)
            sum_shifts(1, 1).then_inc(b_done, 1)
            put_x(1)
            deconv_high(1)
            te.wait_ge(wh_ready, 4)
            te.wait_ge(x2h_ready, IPU)
            conv(0, range(0, 3))
            deconv_low(1)
            conv(0, range(3, TAPS))
            te.wait_ge(x2l_ready, 1)
            conv(1, range(0, 1))
            gn_groups(1, 1)
            conv(1, range(1, TAPS))
            te.wait_ge(wl_ready, 4)
            conv(2).then_inc(conv_done, 1)
            for h in range(IPU):
                conv_image(h).then_inc(conv_done, 1)

        @block.vector
        def _(dve):
            steps = 0

            def link(i):
                nonlocal steps
                i.then_inc(dve_step, 1)
                steps += 1
                dve.wait_ge(dve_step, steps)

            def gn_moments(i, u, src):
                nonlocal steps
                n = norm[i][u]
                for j in range(IPU):
                    dve.bn_stats(n.stats[:, j, :], src[:, j, :]).then_inc(dve_step, 1)
                steps += IPU
                for j in range(IPU):
                    dve.wait_ge(dve_step, steps - IPU + j + 1)
                    a = dve.bn_aggr(n.mv[:, j, :], n.stats[:, j, :])
                a.then_inc(moments, 1)

            def gn_var(i, u, eps):
                n = norm[i][u]
                dve.wait_ge(groups, UNITS * i + u + 1)
                g = gn_ps[u].rearrange("p (i m) -> p i m", m=2)
                link(dve.tensor_tensor(n.dif[:, :], g[:, :, 0], n.mv[:, :, 0], ALU.subtract))
                link(dve.tensor_tensor(n.dif2[:, :], n.dif[:, :], n.dif[:, :], ALU.mult))
                dve.scalar_tensor_tensor(n.var[:, :], n.dif2[:, :], eps, g[:, :, 1],
                                         ALU.add, ALU.add).then_inc(var_ready, 1)
                dve.tensor_copy(n.mean[:, :], g[:, :, 0]).then_inc(mean_ready, 1)
                dve.wait_ge(mean_ready, UNITS * i + u + 1)

            def newton(dst, v, y, a, b, scale):
                link(dve.tensor_tensor(a[:, :], y[:, :], y[:, :], ALU.mult))
                link(dve.scalar_tensor_tensor(b[:, :], a[:, :], -0.5 / scale ** 2, v[:, :], ALU.mult, ALU.mult))
                return dve.scalar_tensor_tensor(dst[:, :], b[:, :], 1.5, y[:, :], ALU.add, ALU.mult)

            def gn_rstd(i, u):
                n = norm[i][u]
                dve.wait_ge(gn_y0, UNITS * i + u + 1)
                link(newton(n.rstd, n.var, n.y0, n.ya, n.yb, F_SCALE))

            def normalise(dst, src, n, j):
                return dve.tensor_scalar(dst, src, n.mean[:, j:j + 1], n.rstd[:, j:j + 1], ALU.subtract, ALU.mult)

            def even(u, j):
                return xh[u][:, j, :].rearrange("p (a r b s) -> p a r b s", a=G, r=2, b=G)[:, :, 0, :, 0]

            def shift_left(t, part):
                return dve.tensor_copy(rows(t[:, 2, of(part), G:G + L])[:, :, :, 0:G - 1],
                                       rows(t[:, 1, of(part), G:G + L])[:, :, :, 1:G])

            def copies_of_f(u, part):
                dve.wait_ge((fh_center, fl_center)[part], u + 1)
                shift_left(fst[u], part).then_inc(f_copied[u][part], 1)
                dve.tensor_copy(inner(fmv[u][half(0), of(part), 0, :]),
                                rows(fst[u][half(0), 1, of(part), G:G + L])).then_inc(f_copied[u][part], 1)

            def high_f(u):
                gn_rstd(0, u)
                for j in range(IPU):
                    i = normalise(rows(fst[u][:, 1, 0:IPU, G:G + L])[:, j], even(u, j), norm[0][u], j)
                i.then_inc(fh_center, 1)
                copies_of_f(u, 0)

            def full_f(u):
                for j in range(IPU):
                    i = normalise(xn[u][:, j, :].rearrange("p (a b) -> p a b", a=G), even(u, j), norm[0][u], j)
                i.then_inc(xn_ready, 1)

            def low_f(u):
                dve.wait_ge(xn_ready, u + 1)
                dve.tensor_tensor(fst[u][:, 1, of(1), G:G + L], xn[u][:, :, :], fst[u][:, 1, of(0), G:G + L],
                                  ALU.subtract).then_inc(fl_center, 1)
                copies_of_f(u, 1)

            def weight_reciprocal(n):
                b, cols = n // 2, slice(n % 2 * TAPS * OC // 2, (n % 2 + 1) * TAPS * OC // 2)
                dve.wait_ge(wden_ready, b + 1)
                dve.reciprocal(wrec[:, b, cols], wden[:, b, cols]).then_inc(wrec_ready, 1)

            inside = slice(1, (G + 2) * G - 1)
            kb = keep_logit[:, :].rearrange("p (i s) -> p i s", i=1).broadcast_to([P, IPU, L])

            def norms(u):
                dve.wait_ge(gram_done, u + 1)
                for j in range(IPU):
                    i = dve.scalar_tensor_tensor(gdiag[u][:, j, :], gram_ps[u][:, j, :], 1.0,
                                                 k_sb[:, K_DIAG:K_DIAG + L], ALU.mult, ALU.mult,
                                                 accum_out=n2[u][:, j:j + 1])
                link(i)
                dve.tensor_scalar(n2c[u][:, :], n2[u][:, :], MIN_NORM2, None, ALU.max).then_inc(n2_ready, 1)

            def inverse_norms(u):
                dve.wait_ge(norm_y0, u + 1)
                newton(rnorm[u], n2c[u], ny0[u], nya[u], nyb[u], Y_SCALE / F_SCALE).then_inc(rnorm_ready, 1)

            def normalise_gram(u):
                dve.wait_ge(rnorm_ready, u + 1)
                r = rnorm[u][:, :].rearrange("p (i s) -> p i s", s=1).broadcast_to([P, IPU, L])
                dve.tensor_tensor(yh[u][:, :, 1:L + 1], gram_ps[u], r, ALU.mult).then_inc(yh_ready, 1)
                dve.tensor_tensor(y32[u][:, :, :], gram_ps[u], r, ALU.mult).then_inc(y32_ready, 1)

            def low_y(u):
                dve.wait_ge(y32_ready, u + 1)
                dve.tensor_tensor(yl[u][:, :, 1:L + 1], y32[u][:, :, :], yh[u][:, :, 1:L + 1],
                                  ALU.subtract).then_inc(yl_ready, 1)

            def low_y1(u):
                dve.wait_ge(eh_ready, u + 1)
                dve.tensor_tensor(el[u][:, :, inside], y1_ps[u][:, :, inside], eh[u][:, :, inside],
                                  ALU.subtract).then_inc(el_ready, 1)

            def logits(u):
                dve.wait_ge(y2_done, u + 1)
                link(dve.tensor_tensor(z[u][:, :, :], y2_ps[u], kb, ALU.mult))
                dve.tensor_reduce(nmax[u][:, :], z[u][:, :, :], AX.X, ALU.max, negate=True).then_inc(z_ready, 1)

            def probabilities(u):
                dve.wait_ge(e_ready, u + 1)
                link(dve.reciprocal(erec[u][:, :], esum[u][:, :]))
                for dst, done in ((pst[u][:, 1, of(0), G:G + L], ph_center), (p32[u][:, :, :], p32_ready)):
                    for j in range(IPU):
                        i = dve.scalar_tensor_tensor(dst[:, j, :], e_sb[u][:, j, :], erec[u][:, j:j + 1],
                                                     keep_prob[:, :], ALU.mult, ALU.mult)
                    i.then_inc(done, 1)
                dve.wait_ge(ph_center, u + 1)
                shift_left(pst[u], 0).then_inc(p_copied[u][0], 1)

            def low_p(u):
                dve.wait_ge(p32_ready, u + 1)
                dve.tensor_tensor(pst[u][:, 1, of(1), G:G + L], p32[u][:, :, :], pst[u][:, 1, of(0), G:G + L],
                                  ALU.subtract).then_inc(pl_center, 1)
                dve.wait_ge(pl_center, u + 1)
                shift_left(pst[u], 1).then_inc(p_copied[u][1], 1)

            def low_ft(u):
                dve.wait_ge(fth_ready, u + 1)
                dve.tensor_tensor(ftl[u][:], ft_ps[u], fth[u][:], ALU.subtract).then_inc(ftl_ready, 1)

            def low_b(u):
                dve.wait_ge(bh_ready, u + 1)
                dve.tensor_tensor(bl[u][:], b_ps[u], bh[u][:], ALU.subtract).then_inc(bl_ready, 1)

            def copy_x1(u, h, r):
                dve.tensor_copy(x1[u][:, h, :].rearrange("p (a r b s) -> p r a b s", a=G, r=2, b=G)[:, r],
                                dec_ps[u][:, h, 2 * r:2 * r + 2, :].rearrange("p s (a b) -> p a b s", a=G)
                                ).then_inc(x1_ready, 1)

            def high_x2(u):
                nonlocal steps
                n = norm[1][u]
                dve.wait_ge(gn_y0, UNITS + u + 1)
                dve.tensor_tensor(n.ya[:, :], n.y0[:, :], n.y0[:, :], ALU.mult).then_inc(dve_step, 1)
                copy_x1(u, 1, 0)
                dve.wait_ge(dve_step, steps + 1)
                dve.scalar_tensor_tensor(n.yb[:, :], n.ya[:, :], -0.5 / F_SCALE ** 2, n.var[:, :],
                                         ALU.mult, ALU.mult).then_inc(dve_step, 1)
                copy_x1(u, 1, 1)
                dve.wait_ge(dve_step, steps + 2)
                steps += 2
                link(dve.scalar_tensor_tensor(n.rstd[:, :], n.yb[:, :], 1.5, n.y0[:, :], ALU.add, ALU.mult))
                dve.wait_ge(zeros_x2, 2 * UNITS)
                dve.wait_ge(x1_ready, 2 * IPU * (u + 1))
                for j in range(IPU):
                    normalise(x2h[u][:, j, 1:H + 1, 1:W + 1], x1[u][:, j, :].rearrange("p (a b) -> p a b", a=H),
                              norm[1][u], j).then_inc(x2h_ready, 1)

            def full_x2(u):
                for j in range(IPU):
                    normalise(x2[u][:, j, :], x1[u][:, j, :], norm[1][u], j).then_inc(x2_ready, 1)

            def low_x2(u, images):
                dve.wait_ge(x2_ready, IPU * u + images.stop)
                dve.tensor_tensor(x2l[u][:, images, 1:H + 1, 1:W + 1],
                                  x2[u][:, images, :].rearrange("p i (a b) -> p i a b", a=H),
                                  x2h[u][:, images, 1:H + 1, 1:W + 1], ALU.subtract).then_inc(x2l_ready, 1)

            for t in fst + fmv:
                dve.memset(flat(t).bitcast(fp32), 0.0).then_inc(zeros_f, 1)
            dve.wait_ge(zeros_f, 2 * UNITS)
            dve.wait_ge(x_in[0], 16)
            gn_moments(0, 0, xh[0])
            gn_var(0, 0, GN_EPS)
            dve.wait_ge(x_in[1], 16)
            gn_moments(0, 1, xh[1])
            high_f(0)
            full_f(0)
            low_f(0)
            gn_var(0, 1, GN_EPS)
            high_f(1)
            dve.wait_ge(k_in, 16)
            dve.wait_ge(zeros_y, 4 * UNITS)
            norms(0)
            full_f(1)
            low_f(1)
            inverse_norms(0)
            normalise_gram(0)
            low_y(0)
            weight_reciprocal(0)
            low_y1(0)
            dve.wait_ge(mask_bc, 1)
            dve.tensor_scalar(keep_logit[:, :], mask_ps, SCALE / Y_SCALE, None, ALU.mult)
            dve.tensor_scalar(keep_prob[:, :], mask_ps, P_SCALE / 4, None, ALU.mult).then_inc(keep_ready, 1)
            norms(1)
            dve.wait_ge(keep_ready, 1)
            logits(0)
            inverse_norms(1)
            normalise_gram(1)
            low_y(1)
            dve.wait_ge(zeros_p, UNITS)
            probabilities(0)
            low_p(0)
            weight_reciprocal(1)
            low_y1(1)
            weight_reciprocal(2)
            logits(1)
            low_ft(0)
            weight_reciprocal(3)
            low_b(0)
            probabilities(1)
            low_p(1)
            dve.wait_ge(dec_done, 1)
            gn_moments(1, 0, x1_ps[0])
            low_ft(1)
            gn_var(1, 0, GN_EPS * X1_SCALE ** 2)
            for r in range(2):
                copy_x1(0, 0, r)
            high_x2(0)
            low_b(1)
            full_x2(0)
            low_x2(0, slice(0, 2))
            dve.wait_ge(dec_done, 2)
            gn_moments(1, 1, x1_ps[1])
            gn_var(1, 1, GN_EPS * X1_SCALE ** 2)
            for r in range(2):
                copy_x1(1, 0, r)
            high_x2(1)
            full_x2(1)
            low_x2(1, slice(0, 1))
            low_x2(1, slice(1, 2))
            for n in range(UNITS * IPU):
                u, h = n // IPU, n % IPU
                dve.wait_ge(conv_done, (1, 1, 2, 3)[n])
                dve.wait_ge(x1b_ready, u + 1)
                px = slice(HW * h, HW * h + HW)
                dve.scalar_tensor_tensor(o_sb[u][:, px], (conv_ps[:, px], conv1_ps[h])[u], 1.0 / (F_SCALE * W_SCALE),
                                         x1b[u][:, px], ALU.mult, ALU.add).then_inc(out_ready, 1)


def kernel(**inputs):
    import concourse.bacc as _bacc
    from concourse.bass_utils import run_bass_kernel_spmd as _run

    a = {k: np.asarray(v) for k, v in inputs.items()}
    c32, k16 = constants()
    copies = P // OC
    weight = np.tile(a["L1_conv_weight"].transpose(1, 2, 3, 0).reshape(OC, TAPS, OC), (copies, 1, 1))
    grids = [np.repeat(a[k].reshape(2, BLOCKS, R).transpose(0, 2, 1), OC, 1).reshape(P, BLOCKS)
             for k in ("L1_conv_alphas", "L1_conv_betas")]
    par = np.concatenate(grids + [np.tile(a["L1_conv_bias"].reshape(C, 1), (2, 1))], 1)
    arrays = {
        "x_in_dram": a["x"].reshape(N, C, HW),
        "mask_in_dram": a["L0_conv_mask"][0:1, 0].reshape(1, MASK_SIDE * MASK_SIDE),
        "weight_in_dram": weight,
        "par_in_dram": par,
        "c32_dram": c32,
        "k16_dram": k16,
    }
    arrays = {k: np.ascontiguousarray(v) for k, v in arrays.items()}
    nc = _bacc.Bacc("TRN2", target_bir_lowering=False, num_devices=1)
    args = [nc.dram_tensor(k, v.shape, mybir.dt.from_np(v.dtype), kind="ExternalInput").ap() for k, v in arrays.items()]
    out = nc.dram_tensor("out_dram", (N, C, HW), mybir.dt.float32, kind="ExternalOutput").ap()
    build(nc, *args, out)
    r = _run(nc, [arrays], core_ids=[0])
    return r.results[0]["out_dram"].reshape(N, C, H, W)
```
